# Optimizing a Trainium2 kernel written in Bass

```python
import numpy as np
import jax
import jax.numpy as jnp

def _softmax(x, axis=-1):
    return jax.nn.softmax(x, axis=axis)

def _gelu(x):
    return jax.nn.gelu(x, approximate=True)

def _silu(x):
    return jax.nn.silu(x)

def _sigmoid(x):
    return jax.nn.sigmoid(x)

def _layernorm(x, axis=-1, eps=1e-05):
    m = jnp.mean(x, axis=axis, keepdims=True)
    v = jnp.var(x, axis=axis, keepdims=True)
    return (x - m) / jnp.sqrt(v + eps)

def _scatter_add(tgt, idx, src, axis=0):
    return tgt.at[idx].add(src)

def _segment_sum(src, seg, n):
    return jax.ops.segment_sum(src, seg, n)
kernel_name = 'mk_macaron_d1_jaxref_r8_ca77e4'

def setup_inputs(seed: int=0):
    np.random.seed(seed)
    _w = jnp.asarray

    def _L0_attn_setup():
        import jax, jax.numpy as jnp
        import numpy as np
        import math
        B, S, D = (4, 256, 256)
        QK = D // 8
        EXP = D * 2
        RESIDUAL_DEPTH = 144
        NUM_BLOCKS = 24
        key = jax.random.key(seed)
        k_x, k_e, k_p = jax.random.split(key, 3)
        x = jax.random.normal(k_x, (B, S, D), jnp.float32)
        expand_scale = 0.5 / math.sqrt(RESIDUAL_DEPTH) / 2.0
        project_scale = 1.0 / math.sqrt(RESIDUAL_DEPTH) / 2.0 / NUM_BLOCKS
        expand = expand_scale * jax.random.normal(k_e, (2 * QK + 2 * EXP, D), jnp.float32)
        project = project_scale * jax.random.normal(k_p, (D, EXP), jnp.float32)
        return {'x': x, 'ln_gamma': jnp.ones((D,), jnp.float32), 'ln_beta': jnp.zeros((D,), jnp.float32), 'expand': expand, 'project': project, 'pos_mult': jnp.float32(1.0)}
    _L0_attn_in = _L0_attn_setup()

    def _L0_ffn_setup():
        import jax, jax.numpy as jnp
        import numpy as np
        B, S, D, H = (4, 256, 256, 1024)

        def fwht(x):
            orig_shape = x.shape
            n = orig_shape[-1]
            x = x.reshape(-1, n)
            h = 1
            while h < n:
                xb = x.reshape(-1, n // (2 * h), 2, h)
                a = xb[:, :, 0, :]
                b = xb[:, :, 1, :]
                x = jnp.stack([a + b, a - b], axis=2).reshape(-1, n)
                h *= 2
            scale = jnp.asarray(1.0 / np.sqrt(n), dtype=x.dtype)
            return (x * scale).reshape(orig_shape)
        key = jax.random.key(seed)
        kx, k1, k2, k3 = jax.random.split(key, 4)
        x = jax.random.normal(kx, (B, S, D), dtype=jnp.float32)
        W1 = jax.random.normal(k1, (H, D), dtype=jnp.float32) * (1.0 / np.sqrt(D))
        W2 = jax.random.normal(k2, (D, H), dtype=jnp.float32) * (1.0 / np.sqrt(H))
        W3 = jax.random.normal(k3, (H, D), dtype=jnp.float32) * (1.0 / np.sqrt(D))
        return {'x': x, 'W1': W1, 'W2': W2, 'W3': W3}
    _L0_ffn_in = _L0_ffn_setup()
    _d = {'L0_attn_x': _L0_attn_in['x'], 'L0_attn_ln_gamma': _L0_attn_in['ln_gamma'], 'L0_attn_ln_beta': _L0_attn_in['ln_beta'], 'L0_attn_expand': _L0_attn_in['expand'], 'L0_attn_project': _L0_attn_in['project'], 'L0_attn_pos_mult': _L0_attn_in['pos_mult'], 'L0_ffn_W1': _L0_ffn_in['W1'], 'L0_ffn_W2': _L0_ffn_in['W2'], 'L0_ffn_W3': _L0_ffn_in['W3']}
    _x0 = _d['L0_attn_x']
    _d['L0_attn_x'] = jax.random.normal(jax.random.fold_in(jax.random.key(seed), 1), (2, 512, 256), dtype=_x0.dtype)
    del _x0
    return _d

def reference(L0_attn_x, L0_attn_ln_gamma, L0_attn_ln_beta, L0_attn_expand, L0_attn_project, L0_attn_pos_mult, L0_ffn_W1, L0_ffn_W2, L0_ffn_W3):

    def _L0_attn_ref(x, ln_gamma, ln_beta, expand, project, pos_mult):
        import jax, jax.numpy as jnp
        import numpy as np
        import math
        B, S, D = (4, 256, 256)
        QK = D // 8
        EXP = D * 2
        RESIDUAL_DEPTH = 144
        NUM_BLOCKS = 24
        Bx, Sx, Dx = x.shape
        qk_dim = Dx // 8
        expand_dim = Dx * 2
        v_dim = Dx
        idx = jnp.arange(Sx)
        rel = (idx[None, :] - idx[:, None]).astype(x.dtype)
        causal = idx[None, :] <= idx[:, None]
        attn_mask = jnp.where(causal, jax.nn.softplus(pos_mult) * rel, -jnp.inf)
        mu = x.mean(-1, keepdims=True)
        var = x.var(-1, keepdims=True)
        h = (x - mu) * jax.lax.rsqrt(var + 1e-05) * ln_gamma + ln_beta
        fused = jnp.einsum('bsd,ed->bse', h, expand)
        query = fused[..., :qk_dim]
        key_ = fused[..., qk_dim:2 * qk_dim]
        linear = fused[..., 2 * qk_dim:2 * qk_dim + expand_dim]
        pre_gelu = fused[..., 2 * qk_dim + expand_dim:]
        geglu = linear * jax.nn.gelu(pre_gelu, approximate=False)
        geglu_local = geglu[..., :expand_dim - v_dim]
        value = geglu[..., expand_dim - v_dim:]
        scale = 1.0 / math.sqrt(qk_dim)
        scores = jnp.einsum('bqd,bkd->bqk', query, key_) * scale + attn_mask
        attn = jnp.einsum('bqk,bkd->bqd', jax.nn.softmax(scores, axis=-1), value)
        out = jnp.einsum('bse,de->bsd', jnp.concatenate([geglu_local, attn], axis=-1), project)
        return x + out

    def _L0_ffn_ref(x, W1, W2, W3):
        import jax, jax.numpy as jnp
        import numpy as np
        B, S, D, H = (4, 256, 256, 1024)

        def fwht(x):
            orig_shape = x.shape
            n = orig_shape[-1]
            x = x.reshape(-1, n)
            h = 1
            while h < n:
                xb = x.reshape(-1, n // (2 * h), 2, h)
                a = xb[:, :, 0, :]
                b = xb[:, :, 1, :]
                x = jnp.stack([a + b, a - b], axis=2).reshape(-1, n)
                h *= 2
            scale = jnp.asarray(1.0 / np.sqrt(n), dtype=x.dtype)
            return (x * scale).reshape(orig_shape)
        up_gate = jnp.einsum('bsd,hd->bsh', x, W1)
        up_lin = jnp.einsum('bsd,hd->bsh', x, W3)
        hidden = jax.nn.silu(up_gate) * up_lin
        hidden = fwht(hidden)
        out = jnp.einsum('bsh,dh->bsd', hidden, W2)
        return out
    x = L0_attn_x
    x = x + 0.5 * _L0_ffn_ref(_layernorm(x, axis=-1), L0_ffn_W1, L0_ffn_W2, L0_ffn_W3)
    x = x + _L0_attn_ref(_layernorm(x, axis=-1), L0_attn_ln_gamma, L0_attn_ln_beta, L0_attn_expand, L0_attn_project, L0_attn_pos_mult)
    x = x + 0.5 * _L0_ffn_ref(_layernorm(x, axis=-1), L0_ffn_W1, L0_ffn_W2, L0_ffn_W3)
    return x

_drawn_inputs = setup_inputs


def setup_inputs(seed=0):
    import zlib

    import numpy as np

    out = dict(_drawn_inputs(seed))
    spreads = {'L0_attn_ln_gamma': (1.0, 0.6), 'L0_attn_ln_beta': (0.0, 0.8)}
    factors = {'L0_attn_expand': 8.0, 'L0_attn_project': 8.0}
    for name, (base, spread) in spreads.items():
        noise = np.random.default_rng([zlib.crc32(name.encode()), seed]).standard_normal(out[name].shape)
        drawn = base * np.exp(spread * noise) if base else spread * noise
        out[name] = jnp.asarray(drawn.astype(out[name].dtype))
    for name, factor in factors.items():
        out[name] = (out[name] * factor).astype(out[name].dtype)
    return out
```

```python
from contextlib import ExitStack

import concourse.bass as bass
from concourse import mybir

P = 128
B, S, D, H = 2, 512, 256, 1024
QK, EXP = D // 8, 2 * D
NT = S // P
KD = D // P
NC = H // P
EPS = 1e-5
SCALE = float(QK) ** -0.5
MASKED = 3.0e38
HIDDEN_SLOTS = NC + 1
GATE_BUFS = 3
COL_Q, COL_K, COL_LOC, COL_VAL = 0, P, 2 * P, 2 * P + 4 * P
EXPAND_COLS = COL_VAL + 2 * D
SPLIT = 512
N_EXPAND_SPLITS = KD * EXPAND_COLS // SPLIT
N_PROJ_SPLITS = (EXP // P) * D // SPLIT

F32 = mybir.dt.float32
F32R = mybir.dt.float32r
ALU = mybir.AluOpType
ACT = mybir.ActivationFunctionType


def steps():
    order = [("t", 0, 0, t) for t in range(NT)]
    for f in range(2):
        for c in range(NC):
            order.append(("up", f, 0, c))
            if (f, c) == (1, 0):
                order += [("out", f, 1, t) for t in range(NT)]
            if f == 0 and c == 4 or f == 1 and c == 6:
                order += [("t", 2 * f, 1, t) for t in range(NT)]
        if f == 0:
            order += [("had", 0, 0, g) for g in range(4)]
        order.append(("up", f, 1, 0))
        order += [("down", f, 0, t) for t in range(NT)]
        for c in range(1, NC):
            order.append(("up", f, 1, c))
            if f == 0 and c == 6:
                order += [("t", 1, 0, t) for t in range(NT)]
        order += [("down", f, 1, t) for t in range(NT)]
        if f == 0:
            order += [("q", 0, 0, 0), ("k", 0, 0, 0)]
            order += [("loc", 0, 0, e) for e in range(KD)]
            order += [("score", 0, 0, i) for i in range(NT)]
            order += [("val", 0, 0, t) for t in range(NT)]
            order += [("t", 1, 1, t) for t in range(NT)]
            order += [("q", 0, 1, 0), ("k", 0, 1, 0)]
            order += [("pt", 0, 0, i) for i in range(NT)]
            order += [("loc", 0, 1, e) for e in range(KD)]
            order += [("score", 0, 1, i) for i in range(NT)]
            order += [("av", 0, 0, e) for e in range(KD)]
            order += [("val", 0, 1, t) for t in range(NT)]
            order += [("out", 0, 0, t) for t in range(NT)]
            order += [("pt", 0, 1, i) for i in range(NT)]
            order += [("av", 0, 1, e) for e in range(KD)]
            order += [("t", 2, 0, t) for t in range(NT)]
    return [("out", 0, b, i) if k == "out" else (k, f, b, i) for k, f, b, i in order]


STEPS = steps()


def numbered(kinds):
    return {s: n for n, s in enumerate(s for s in STEPS if s[0] in kinds)}


GATES = numbered({"up", "loc", "val"})
NORMED = numbered({"t"})
ACCS = numbered({"had", "down", "score", "out"})
SUMS = numbered({"down", "out"})
SOFT = numbered({"pt"})


def ring_places():
    at, places = 0, {}
    for s in STEPS:
        if s[0] in ("up", "loc"):
            places[s] = at
            at += 2
        elif s[0] in ("t", "q", "k", "val", "pt", "av"):
            places[s] = at
            at += 1
    return places


RING = ring_places()


def banks_of(s):
    return 2 if s[0] in ("up", "loc") else 1


def ring_end(s):
    return RING[s] + banks_of(s)


def occupants(s):
    first = RING[s] - 4
    return [r for r in RING if RING[r] < first + banks_of(s) and ring_end(r) > max(first, 0)] if first + banks_of(s) > 0 else []


def gate_slot(s):
    _, _, b, c = s
    return c if b == 0 else (NC if c == 0 else c - 1)


STATS = [("ffn0", 0), ("ffn0", 1), ("outer", 0), ("inner", 0), ("outer", 1), ("inner", 1),
         ("ffn1", 0), ("ffn1", 1)]


def stat(kind, b, t):
    return STATS.index((kind, b)) * NT + t


def build_macaron(nc, x_d, w13_d, w2_d, expand_d, proj_d, const_d, gb_d, pos_d, out_d):
    with ExitStack() as ctx:
        def sb(name, shape, dt=F32):
            return ctx.enter_context(nc.sbuf_tensor(name, shape, dt))

        def sem(name):
            return ctx.enter_context(nc.semaphore(name))

        X = sb("residual", [P, B, NT, D])
        w13_raw = sb("w13_raw", [P, 4, 2 * KD * P])
        logits = w13_raw
        with nc.sbuf_tensor("w2_raw", [P, 2, NC * D], F32) as w2_raw:
            pass
        PT = sb("probs_T", [P, 2, NT, S], F32R)
        att_raw = w2_raw[:, :, :].rearrange("p a n -> p (a n)")
        W13 = sb("w13_split", [P, NC, 2, 2 * KD * P], F32R)
        W2 = sb("w2_split", [P, NC, 2, D], F32R)
        w2s = sb("w2_prod_split", [P, 2, NC * D], F32R)
        V = w2s[:, :, :].rearrange("p h (b t d) -> p b t h d", b=B, t=NT)
        WE = sb("expand_split", [P, 2, KD * EXPAND_COLS], F32R)
        WP = sb("proj_split", [P, EXP // P, 2, D], F32R)
        XT = sb("normed_T", [P, B, 2, KD, S], F32R)
        HID = sb("hidden_T", [P, HIDDEN_SLOTS, 2, S], F32R)
        QKS = sb("qk_rows", [P, 2, S], F32R)
        gated = sb("gated", [P, GATE_BUFS, S])
        xp = sb("outer_norm", [P, NT, D])
        normed = sb("normed", [P, NT, D])
        hfull = sb("affine_T", [P, 2, D])
        bias = sb("position_bias", [P, S])
        const = sb("const", [P, 2 * P + 2])
        ident, had = const[:, 0:P], const[:, P:2 * P]
        qmask, kmask = const[:, 2 * P:2 * P + 1], const[:, 2 * P + 1:2 * P + 2]
        HADR = sb("hadamard", [P, P], F32R)
        gb = sb("gamma_beta", [P, 2 * KD])
        NS = len(STATS) * NT
        bn = sb("bn", [P, NS, 6])
        mv = sb("mean_var", [P, NS, 2])
        ve = sb("var_eps", [P, NS])
        rstd = sb("rstd", [P, NS])
        minus_half = sb("minus_half", [P, 1])
        pos = sb("pos", [P, 6])
        soft = sb("soft_stats", [P, B * NT, 3])

        ring = ctx.enter_context(nc.psum_tensor("ring", [P, 4, 512], F32))
        acc = ctx.enter_context(nc.psum_tensor("acc", [P, 4, 512], F32))

        x_in = [[sem(f"x_in{b}{t}") for t in range(NT)] for b in range(B)]
        w13_in = [sem(f"w13_in{c}") for c in range(NC)]
        w2_in, expand_in, proj_in = sem("w2_in"), sem("expand_in"), sem("proj_in")
        const_in, gb_in, pos_in, out_done = sem("const_in"), sem("gb_in"), sem("pos_in"), sem("out_done")
        ring_full, acc_full = sem("ring_full"), sem("acc_full")
        w13_hi, w13_split = sem("w13_hi"), sem("w13_split")
        w2_mixed, w2s_hi, w2s_split = sem("w2_mixed"), sem("w2s_hi"), sem("w2s_split")
        w2_hi, w2_lo, had_ready = sem("w2_hi"), sem("w2_lo"), sem("had_ready")
        att_hi, att_split = sem("att_hi"), sem("att_split")
        act_ready, gate_ready, gate_hi, gate_lo = sem("act_ready"), sem("gate_ready"), sem("gate_hi"), sem("gate_lo")
        bn_done, mv_done, var_ready, rstd_ready = sem("bn_done"), sem("mv_done"), sem("var_ready"), sem("rstd_ready")
        outer_ready, outer_added, normed_ready = sem("outer_ready"), sem("outer_added"), sem("normed_ready")
        affine_ready, xt_hi, xt_lo = sem("affine_ready"), sem("xt_hi"), sem("xt_lo")
        half_added, x_done = sem("half_added"), sem("x_done")
        qk_hi, qk_rows = sem("qk_hi"), sem("qk_rows_ready")
        logits_ready, exp_ready, recip_ready, probs_ready = sem("logits_ready"), sem("exp_ready"), sem("recip_ready"), sem("probs_ready")
        pt_hi, pt_lo, av_hi, av_lo = sem("pt_hi"), sem("pt_lo"), sem("av_hi"), sem("av_lo")
        bias_ready, rel_ready, half_ready = sem("bias_ready"), sem("rel_ready"), sem("half_ready")
        pos_abs, pos_exp, pos_ln, pos_slope = sem("pos_abs"), sem("pos_exp"), sem("pos_ln"), sem("pos_slope")

        def ring_bank(s, n=0):
            return ring[:, (RING[s] + n) % 4]

        def acc_bank(s):
            return acc[:, ACCS[s] % 4]

        def acc_end(s):
            return ACCS[s] + 1

        def gate_dst(s, part):
            kind, _, b, i = s
            if kind == "up":
                return HID[:, gate_slot(s), part, :]
            if kind == "loc":
                return HID[:, 4 * b + i, part, :]
            return V[:, b, i, part, :]

        def gate_width(s):
            return D if s[0] == "val" else S

        def gate_dst_free(eng, s):
            kind, f, b, i = s
            if kind == "up" and b == 1 and i > 0:
                eng.wait_ge(acc_full, acc_end(("down", f, 0, NT - 1)))
            elif kind == "up" and f == 1:
                eng.wait_ge(acc_full, acc_end(("out", 0, 1 if (b, i) >= (0, 4) else 0, NT - 1)))
            elif kind in ("loc",):
                eng.wait_ge(acc_full, acc_end(("down", 0, 1, NT - 1)))
            elif kind == "val":
                eng.wait_ge(acc_full, acc_end(("had", 0, 0, 3)))

        def xt_free(eng, s):
            _, n, b, _ = s
            if n:
                last = ("up", 0, b, NC - 1) if n == 1 else ("val", 0, b, NT - 1)
                eng.wait_ge(ring_full, ring_end(last))

        def released_by(s):
            kind, f, b, i = s
            if kind in ("up", "loc", "val"):
                return gate_ready, GATES[s] + 1
            if kind == "t":
                return (affine_ready, KD * (NT * b + i + 1)) if f == 1 else (xt_lo, NORMED[s] + 1)
            if kind in ("q", "k"):
                return qk_rows, 2 * b + (1 if kind == "q" else 2)
            if kind == "pt":
                return pt_lo, SOFT[s] + 1
            if kind == "av":
                return av_lo, KD * b + i + 1
            if kind == "had":
                return w2_lo, i + 1
            if kind == "score":
                return logits_ready, NT * b + i + 1
            return x_done, SUMS[s] + 1

        block = ctx.enter_context(nc.Block())

        @block.sync
        def _(sp):
            def load_x(b, t):
                sp.dma_start(X[:, b, t], x_d[b, t * P:(t + 1) * P, :]).then_inc(x_in[b][t], 16)

            def load_w13(c):
                if c >= 4:
                    sp.wait_ge(w13_split, c - 3)
                sp.dma_start(w13_raw[:, c % 4], w13_d[c]).then_inc(w13_in[c], 16)

            for t in range(NT):
                load_x(0, t)
            load_w13(1)
            sp.dma_start(w2_raw[:, 0], w2_d).then_inc(w2_in, 16)
            load_w13(2)
            load_w13(3)
            for t in range(NT):
                load_x(1, t)
            for c in range(4, NC):
                load_w13(c)
            sp.wait_ge(w2s_split, 4)
            sp.dma_start(att_raw[:, 0:KD * EXPAND_COLS], expand_d).then_inc(expand_in, 16)
            sp.dma_start(att_raw[:, KD * EXPAND_COLS:KD * EXPAND_COLS + EXP // P * D], proj_d).then_inc(proj_in, 16)
            for b in range(B):
                for t in range(NT):
                    sp.wait_ge(x_done, NT * (4 + b) + t + 1)
                    sp.dma_start(out_d[b, t * P:(t + 1) * P, :], X[:, b, t]).then_inc(out_done, 16)
            sp.wait_ge(out_done, 16 * B * NT)

        @block.gpsimd
        def _(pool):
            nc.gpsimd.memset(minus_half[:], -0.5).then_inc(half_ready, 1)
            nc.gpsimd.iota(bias[:], pattern=[[-1, S]], base=S - P, channel_multiplier=1,
                           allow_small_or_imprecise_dtypes=True).then_inc(rel_ready, 1)
            pool.wait_ge(half_ready, 1)

            def reciprocal_roots(kind, b):
                for t in range(NT):
                    n = stat(kind, b, t)
                    pool.wait_ge(var_ready, n + 1)
                    nc.gpsimd.tensor_tensor(rstd[:, n:n + 1], ve[:, n:n + 1], minus_half[:], ALU.pow)\
                        .then_inc(rstd_ready, 1)

            def add_outer(b):
                for t in range(NT):
                    pool.wait_ge(outer_ready, NT * b + t + 1)
                    nc.gpsimd.tensor_tensor(X[:, b, t], X[:, b, t], xp[:, t], ALU.add).then_inc(outer_added, 1)

            reciprocal_roots("ffn0", 0)
            pool.wait_ge(w2_in, 16)
            for stage in range(3):
                h = 1 << stage
                src = w2_raw[:, stage % 2].rearrange("p (g two r) -> p g two r", two=2, r=h * D)
                dst = w2_raw[:, 1 - stage % 2].rearrange("p (g two r) -> p g two r", two=2, r=h * D)
                if stage:
                    pool.wait_ge(w2_mixed, 2 * stage)
                nc.gpsimd.tensor_tensor(dst[:, :, 0], src[:, :, 0], src[:, :, 1], ALU.add).then_inc(w2_mixed, 1)
                nc.gpsimd.tensor_tensor(dst[:, :, 1], src[:, :, 0], src[:, :, 1], ALU.subtract).then_inc(w2_mixed, 1)
                if stage == 0:
                    reciprocal_roots("ffn0", 1)
            for b in range(B):
                reciprocal_roots("outer", b)
                reciprocal_roots("inner", b)
                add_outer(b)
                if b == 0:
                    pool.wait_ge(rel_ready, 1)
                    pool.wait_ge(pos_slope, 3)
                    nc.gpsimd.tensor_scalar(bias[:], bias[:], pos[:, 5:6], None, ALU.mult).then_inc(rel_ready, 1)
                    pool.wait_ge(rel_ready, 2)
                    nc.gpsimd.affine_select(out=bias[:], in_=bias[:], compare_op=ALU.is_ge, fill=MASKED,
                                            base=S - P, pattern=[[-1, S]], channel_multiplier=1)\
                        .then_inc(bias_ready, 1)
            reciprocal_roots("ffn1", 0)
            reciprocal_roots("ffn1", 1)

        @block.scalar
        def _(act):
            act.dma_start(w13_raw[:, 0], w13_d[0]).then_inc(w13_in[0], 16)
            act.dma_start(const[:], const_d).then_inc(const_in, 16)
            act.dma_start(gb[:], gb_d).then_inc(gb_in, 16)
            act.dma_start(pos[:, 0:1], pos_d.to_broadcast([P, 1])).then_inc(pos_in, 16)

            def split_w13(c):
                act.wait_ge(w13_in[c], 16)
                nc.scalar.activation(W13[:, c, 0], w13_raw[:, c % 4], ACT.Copy).then_inc(w13_hi, 1)

            def split_w2s(n):
                if n == 0:
                    act.wait_ge(w2_mixed, 6)
                r = slice(n * SPLIT, (n + 1) * SPLIT)
                nc.scalar.activation(w2s[:, 0, r], w2_raw[:, 1, r], ACT.Copy).then_inc(w2s_hi, 1)

            def split_att(n):
                act.wait_ge(expand_in if n < N_EXPAND_SPLITS else proj_in, 16)
                src = att_raw[:, n * SPLIT:(n + 1) * SPLIT]
                if n < N_EXPAND_SPLITS:
                    dst = WE[:, 0, n * SPLIT:(n + 1) * SPLIT]
                else:
                    m = n - N_EXPAND_SPLITS
                    dst = WP[:, 2 * m:2 * m + 2, 0, :]
                    src = src.rearrange("p (e d) -> p e d", d=D)
                nc.scalar.activation(dst, src, ACT.Copy).then_inc(att_hi, 1)

            def gate_activation(s):
                n, w = GATES[s], gate_width(s)
                act.wait_ge(ring_full, RING[s] + 1)
                if n >= GATE_BUFS:
                    act.wait_ge(gate_lo, n - GATE_BUFS + 1)
                nc.scalar.activation(gated[:, n % GATE_BUFS, 0:w], ring_bank(s)[:, 0:w],
                                     ACT.Silu if s[0] == "up" else ACT.Gelu).then_inc(act_ready, 1)

            def gate_high(s):
                n = GATES[s]
                act.wait_ge(gate_ready, n + 1)
                gate_dst_free(act, s)
                nc.scalar.activation(gate_dst(s, 0), gated[:, n % GATE_BUFS, 0:gate_width(s)], ACT.Copy)\
                    .then_inc(gate_hi, 1)

            def position_slope():
                act.wait_ge(pos_abs, 2)
                nc.scalar.activation(pos[:, 2:3], pos[:, 1:2], ACT.Exp, scale=-1.0).then_inc(pos_exp, 1)
                act.wait_ge(pos_exp, 1)
                nc.scalar.activation(pos[:, 3:4], pos[:, 2:3], ACT.Ln, bias=1.0).then_inc(pos_ln, 1)

            def exponentials(b):
                for i in range(NT):
                    n = NT * b + i
                    act.wait_ge(logits_ready, n + 1)
                    row = logits[:, i, 0:(i + 1) * P]
                    nc.scalar.activation(row, row, ACT.Exp, scale=-1.0, bias=soft[:, n, 0:1],
                                         accum_out=soft[:, n, 1:2]).then_inc(exp_ready, 1)

            def transposed_high(s):
                _, f, b, i = s
                xt_free(act, s)
                if f == 1:
                    a = NT * b + i
                    act.wait_ge(affine_ready, KD * (a + 1))
                    src = hfull[:, a % 2]
                else:
                    act.wait_ge(ring_full, ring_end(s))
                    src = ring_bank(s)[:, 0:D]
                nc.scalar.activation(XT[:, b, 0, :, i * P:(i + 1) * P], src.rearrange("p (k m) -> p k m", k=KD),
                                     ACT.Copy).then_inc(xt_hi, 1)

            split_w13(0)
            split_w13(1)
            act.wait_ge(const_in, 16)
            nc.scalar.activation(HADR[:], had, ACT.Copy).then_inc(had_ready, 1)
            for s in STEPS:
                kind, f, b, i = s
                if kind in ("up", "loc", "val"):
                    gate_activation(s)
                    if (kind, f, b) == ("up", 0, 0) and i + 2 < NC:
                        split_w13(i + 2)
                    gate_high(s)
                if (kind, f, b) == ("up", 0, 0) and i == NC - 1:
                    for n in range(NC * D // SPLIT):
                        split_w2s(n)
                if (kind, f, b) == ("up", 0, 1) and i >= 1:
                    split_att(i - 1)
                if kind == "t":
                    transposed_high(s)
                if kind == "had":
                    act.wait_ge(acc_full, acc_end(s))
                    nc.scalar.activation(W2[:, 2 * i:2 * i + 2, 0, :],
                                         acc_bank(s).rearrange("p (c d) -> p c d", d=D), ACT.Copy).then_inc(w2_hi, 1)
                if kind in ("q", "k"):
                    act.wait_ge(ring_full, ring_end(s))
                    if b:
                        act.wait_ge(acc_full, acc_end(("score", 0, 0, NT - 1)))
                    which = 0 if kind == "q" else 1
                    nc.scalar.activation(QKS[:, which], ring_bank(s), ACT.Copy,
                                         scale=-1.0 if kind == "q" else 1.0).then_inc(qk_hi, 1)
                if kind == "pt":
                    act.wait_ge(ring_full, ring_end(s))
                    if b:
                        act.wait_ge(ring_full, ring_end(("av", 0, 0, KD - 1)))
                    nc.scalar.activation(PT[:, 0, 0:i + 1, i * P:(i + 1) * P],
                                         ring_bank(s)[:, 0:(i + 1) * P].rearrange("p (j q) -> p j q", q=P),
                                         ACT.Copy).then_inc(pt_hi, 1)
                if kind == "av":
                    act.wait_ge(ring_full, ring_end(s))
                    nc.scalar.activation(HID[:, NT * b + KD + i, 0, :], ring_bank(s), ACT.Copy).then_inc(av_hi, 1)
                if s == ("down", 0, 1, 0):
                    position_slope()
                if kind == "val" and i == NT - 1:
                    exponentials(b)

        @block.vector
        def _(dve):
            def split_w13(c):
                dve.wait_ge(w13_hi, c + 1)
                nc.vector.tensor_tensor(W13[:, c, 1], w13_raw[:, c % 4], W13[:, c, 0].bitcast(F32),
                                        ALU.subtract).then_inc(w13_split, 1)

            def split_w2s(n):
                dve.wait_ge(w2s_hi, n + 1)
                r = slice(n * SPLIT, (n + 1) * SPLIT)
                nc.vector.tensor_tensor(w2s[:, 1, r], w2_raw[:, 1, r], w2s[:, 0, r].bitcast(F32),
                                        ALU.subtract).then_inc(w2s_split, 1)

            def split_att(n):
                dve.wait_ge(att_hi, n + 1)
                src = att_raw[:, n * SPLIT:(n + 1) * SPLIT]
                if n < N_EXPAND_SPLITS:
                    hi, lo = (WE[:, h, n * SPLIT:(n + 1) * SPLIT] for h in range(2))
                else:
                    m = n - N_EXPAND_SPLITS
                    hi, lo = (WP[:, 2 * m:2 * m + 2, h, :] for h in range(2))
                    src = src.rearrange("p (e d) -> p e d", d=D)
                nc.vector.tensor_tensor(lo, src, hi.bitcast(F32), ALU.subtract).then_inc(att_split, 1)

            def statistics(kind, b, src):
                for t in range(NT):
                    if kind == "ffn0":
                        dve.wait_ge(x_in[b][t], 16)
                    n = stat(kind, b, t)
                    nc.vector.bn_stats(bn[:, n], src(t)).then_inc(bn_done, 1)
                for t in range(NT):
                    n = stat(kind, b, t)
                    dve.wait_ge(bn_done, n + 1)
                    nc.vector.bn_aggr(mv[:, n], bn[:, n]).then_inc(mv_done, 1)
                for t in range(NT):
                    n = stat(kind, b, t)
                    dve.wait_ge(mv_done, n + 1)
                    nc.vector.tensor_scalar(ve[:, n:n + 1], mv[:, n, 1:2], EPS, None, ALU.add).then_inc(var_ready, 1)

            def normalize(kind, b, t, dst, src):
                n = stat(kind, b, t)
                dve.wait_ge(rstd_ready, n + 1)
                return nc.vector.tensor_scalar(dst, src, mv[:, n, 0:1], rstd[:, n:n + 1], ALU.subtract, ALU.mult)

            def normed_free(s):
                n = NORMED[s]
                if n >= NT:
                    before = next(r for r in NORMED if NORMED[r] == n - NT)
                    dve.wait_ge(ring_full, ring_end(before))

            def ffn_statistics(f, b):
                if f:
                    dve.wait_ge(x_done, SUMS[("out", 0, b, NT - 1)] + 1)
                statistics(f"ffn{f}", b, lambda t: X[:, b, t])

            def ffn_normalize(f, b):
                for t in range(NT):
                    normed_free(("t", 2 * f, b, t))
                    normalize(f"ffn{f}", b, t, normed[:, t], X[:, b, t]).then_inc(normed_ready, 1)

            def outer_statistics(b):
                dve.wait_ge(x_done, SUMS[("down", 0, b, NT - 1)] + 1)
                statistics("outer", b, lambda t: X[:, b, t])

            def outer_normalize(b):
                for t in range(NT):
                    if b:
                        dve.wait_ge(outer_added, t + 1)
                    normalize("outer", b, t, xp[:, t], X[:, b, t]).then_inc(outer_ready, 1)

            def inner_statistics(b):
                dve.wait_ge(outer_ready, NT * (b + 1))
                statistics("inner", b, lambda t: xp[:, t])

            def inner_normalize(b):
                for t in range(NT):
                    normed_free(("t", 1, b, t))
                    normalize("inner", b, t, normed[:, t], xp[:, t]).then_inc(normed_ready, 1)

            def position_magnitude():
                dve.wait_ge(pos_in, 16)
                nc.vector.tensor_scalar(pos[:, 4:5], pos[:, 0:1], -1.0, None, ALU.mult).then_inc(pos_abs, 1)
                dve.wait_ge(pos_abs, 1)
                nc.vector.tensor_tensor(pos[:, 1:2], pos[:, 0:1], pos[:, 4:5], ALU.max).then_inc(pos_abs, 1)

            def position_slope():
                dve.wait_ge(pos_ln, 1)
                nc.vector.tensor_scalar(pos[:, 4:5], pos[:, 0:1], 0.0, None, ALU.max).then_inc(pos_slope, 1)
                dve.wait_ge(pos_slope, 1)
                nc.vector.tensor_tensor(pos[:, 5:6], pos[:, 4:5], pos[:, 3:4], ALU.add).then_inc(pos_slope, 1)
                dve.wait_ge(pos_slope, 2)
                nc.vector.tensor_scalar(pos[:, 5:6], pos[:, 5:6], 1.0 / SCALE, None, ALU.mult).then_inc(pos_slope, 1)

            def gate(s):
                n, w = GATES[s], gate_width(s)
                linear = ring_bank(s)[:, D:2 * D] if s[0] == "val" else ring_bank(s, 1)
                tile = gated[:, n % GATE_BUFS, 0:w]
                dve.wait_ge(act_ready, n + 1)
                dve.wait_ge(ring_full, ring_end(s))
                nc.vector.tensor_tensor(tile, tile, linear, ALU.mult).then_inc(gate_ready, 1)
                dve.wait_ge(gate_hi, n + 1)
                nc.vector.tensor_tensor(gate_dst(s, 1), tile, gate_dst(s, 0).bitcast(F32), ALU.subtract)\
                    .then_inc(gate_lo, 1)

            def transposed_low(s):
                _, f, b, i = s
                n, a = NORMED[s], NT * b + i
                source = ring_bank(s)[:, 0:D]
                dve.wait_ge(ring_full, ring_end(s))
                if f == 1:
                    if a >= 2:
                        dve.wait_ge(xt_lo, n - 1)
                    for k in range(KD):
                        c = slice(k * P, (k + 1) * P)
                        nc.vector.tensor_scalar(hfull[:, a % 2, c], source[:, c], gb[:, k:k + 1],
                                                gb[:, KD + k:KD + k + 1], ALU.mult, ALU.add).then_inc(affine_ready, 1)
                    source = hfull[:, a % 2]
                    dve.wait_ge(affine_ready, KD * (a + 1))
                dve.wait_ge(xt_hi, n + 1)
                c = slice(i * P, (i + 1) * P)
                nc.vector.tensor_tensor(XT[:, b, 1, :, c], source.rearrange("p (k m) -> p k m", k=KD),
                                        XT[:, b, 0, :, c].bitcast(F32), ALU.subtract).then_inc(xt_lo, 1)

            def qk_low(s):
                kind, _, b, _ = s
                n = 2 * b + (kind == "k")
                part, mask = QKS[:, n % 2], (qmask, kmask)[n % 2]
                dve.wait_ge(qk_hi, n + 1)
                nc.vector.scalar_tensor_tensor(part, part.bitcast(F32), mask, ring_bank(s), ALU.mult,
                                               ALU.subtract if kind == "q" else ALU.add).then_inc(qk_rows, 1)

            def negated_logits(s):
                _, _, b, i = s
                w = (i + 1) * P
                dve.wait_ge(acc_full, acc_end(s))
                if b == 0 and i == 0:
                    dve.wait_ge(bias_ready, 1)
                    dve.wait_ge(w13_split, NC)
                if b:
                    dve.wait_ge(ring_full, ring_end(("pt", 0, 0, i)))
                nc.vector.tensor_tensor_reduce(out=logits[:, i, 0:w], in0=acc_bank(s)[:, 0:w],
                                               in1=bias[:, S - w:S], scale=SCALE, scalar=MASKED, op0=ALU.add,
                                               op1=ALU.min, accum_out=soft[:, NT * b + i, 0:1]).then_inc(logits_ready, 1)

            def probabilities(b, i):
                n = NT * b + i
                row = logits[:, i, 0:(i + 1) * P]
                dve.wait_ge(exp_ready, n + 1)
                nc.vector.reciprocal(soft[:, n, 2:3], soft[:, n, 1:2]).then_inc(recip_ready, 1)
                dve.wait_ge(recip_ready, n + 1)
                nc.vector.tensor_scalar(row, row, soft[:, n, 2:3], None, ALU.mult).then_inc(probs_ready, 1)

            def add_product(s):
                kind, _, b, t = s
                dve.wait_ge(acc_full, acc_end(s))
                if kind == "out":
                    dve.wait_ge(outer_added, NT * b + t + 1)
                nc.vector.tensor_tensor(X[:, b, t], X[:, b, t], acc_bank(s)[:, 0:D], ALU.add).then_inc(half_added, 1)
                dve.wait_ge(half_added, SUMS[s] + 1)
                nc.vector.tensor_tensor(X[:, b, t], X[:, b, t], acc_bank(s)[:, D:2 * D], ALU.add).then_inc(x_done, 1)

            ffn_statistics(0, 0)
            ffn_normalize(0, 0)
            split_w13(0)
            split_w13(1)
            dve.wait_ge(gb_in, 16)
            for s in STEPS:
                kind, f, b, i = s
                if kind in ("up", "loc", "val"):
                    gate(s)
                if (kind, f, b) == ("up", 0, 0):
                    if i + 2 < NC:
                        split_w13(i + 2)
                    if i == 0:
                        ffn_statistics(0, 1)
                    if i == 3:
                        ffn_normalize(0, 1)
                    if i == 5:
                        position_magnitude()
                    if i == NC - 1:
                        for n in range(NC * D // SPLIT):
                            split_w2s(n)
                if kind == "t":
                    transposed_low(s)
                if kind == "had":
                    dve.wait_ge(w2_hi, i + 1)
                    nc.vector.tensor_tensor(W2[:, 2 * i:2 * i + 2, 1, :],
                                            acc_bank(s).rearrange("p (c d) -> p c d", d=D),
                                            W2[:, 2 * i:2 * i + 2, 0, :].bitcast(F32), ALU.subtract).then_inc(w2_lo, 1)
                if (kind, f, b) == ("up", 0, 1) and i >= 1:
                    split_att(i - 1)
                if kind in ("down", "out"):
                    add_product(s)
                if kind in ("q", "k"):
                    qk_low(s)
                if kind == "score":
                    negated_logits(s)
                if kind == "pt":
                    dve.wait_ge(pt_hi, SOFT[s] + 1)
                    high, low = (PT[:, h, 0:i + 1, i * P:(i + 1) * P] for h in range(2))
                    nc.vector.tensor_tensor(low, ring_bank(s)[:, 0:(i + 1) * P].rearrange("p (j q) -> p j q", q=P),
                                            high.bitcast(F32), ALU.subtract).then_inc(pt_lo, 1)
                if kind == "av":
                    dve.wait_ge(av_hi, KD * b + i + 1)
                    high, low = (HID[:, NT * b + KD + i, h, :] for h in range(2))
                    nc.vector.tensor_tensor(low, ring_bank(s), high.bitcast(F32), ALU.subtract).then_inc(av_lo, 1)
                if s == ("down", 0, 0, NT - 1):
                    outer_statistics(0)
                if s == ("up", 0, 1, 1):
                    outer_normalize(0)
                    inner_statistics(0)
                if s == ("up", 0, 1, 3):
                    inner_normalize(0)
                if s == ("down", 0, 1, 0):
                    position_slope()
                if s == ("down", 0, 1, NT - 1):
                    outer_statistics(1)
                if s == ("k", 0, 0, 0):
                    outer_normalize(1)
                    inner_statistics(1)
                if s == ("loc", 0, 0, KD - 1):
                    inner_normalize(1)
                if s == ("k", 0, 1, 0):
                    for i in range(NT):
                        probabilities(0, i)
                if kind == "out" and b == 0:
                    probabilities(1, i)
                if s == ("out", 0, 0, NT - 1):
                    ffn_statistics(1, 0)
                if s == ("pt", 0, 1, 1):
                    ffn_normalize(1, 0)
                if s == ("out", 0, 1, NT - 1):
                    ffn_statistics(1, 1)
                if s == ("up", 1, 0, 1):
                    ffn_normalize(1, 1)

        @block.tensor
        def _(pe):
            def mm(out, stationary, moving, start, stop):
                return nc.tensor.matmul(out, stationary, moving, start=start, stop=stop)

            def three(out, stationary, moving, start, stop):
                mm(out, stationary(0), moving(0), start, False)
                mm(out, stationary(0), moving(1), False, False)
                return mm(out, stationary(1), moving(0), False, stop)

            def token_product(out, slots, weights):
                last = len(slots) - 1
                for n, rows in enumerate(slots):
                    mm(out, rows(0), weights(n)[:, 0:2 * D], n == 0, False)
                    ins = mm(out[:, 0:D], rows(1), weights(n)[:, 0:D], False, n == last)
                return ins

            def bank_free(s):
                if s in RING:
                    before = occupants(s)
                else:
                    before = [r for r in ACCS if ACCS[r] == ACCS[s] - 4]
                for r in before:
                    pe.wait_ge(*released_by(r))

            for s in STEPS:
                kind, f, b, i = s
                bank_free(s)
                if kind == "t":
                    if s == ("t", 0, 0, 0):
                        pe.wait_ge(const_in, 16)
                    pe.wait_ge(normed_ready, NORMED[s] + 1)
                    for k in range(KD):
                        c = slice(k * P, (k + 1) * P)
                        ins = nc.tensor.transpose(ring_bank(s)[:, c], normed[:, i, c], ident)
                    ins.then_inc(ring_full, 1)
                if kind == "up":
                    pe.wait_ge(xt_lo, NORMED[("t", 2 * f, b, NT - 1)] + 1)
                    pe.wait_ge(w13_split, i + 1)
                    for w in range(2):
                        for k in range(KD):
                            c = slice((w * KD + k) * P, (w * KD + k + 1) * P)
                            ins = three(ring_bank(s, w), lambda h: W13[:, i, h, c], lambda h: XT[:, b, h, k],
                                        k == 0, k == KD - 1)
                        ins.then_inc(ring_full, 1)
                if kind == "had":
                    pe.wait_ge(had_ready, 1)
                    pe.wait_ge(w2s_split, i + 1)
                    r = slice(i * SPLIT, (i + 1) * SPLIT)
                    mm(acc_bank(s), HADR[:], w2s[:, 0, r], True, False)
                    mm(acc_bank(s), HADR[:], w2s[:, 1, r], False, True).then_inc(acc_full, 1)
                if kind == "down":
                    pe.wait_ge(w2_lo, 4)
                    pe.wait_ge(gate_lo, GATES[("up", f, b, NC - 1)] + 1 if b == 0 or i == 0 else 1)
                    t = slice(i * P, (i + 1) * P)
                    token_product(acc_bank(s),
                                  [lambda h, c=c: HID[:, gate_slot(("up", f, b, c)), h, t] for c in range(NC)],
                                  lambda c: W2[:, c].rearrange("p h d -> p (h d)")).then_inc(acc_full, 1)
                if kind in ("q", "k", "loc", "val"):
                    pe.wait_ge(xt_lo, NORMED[("t", 1, b, NT - 1)] + 1)
                    pe.wait_ge(att_split, N_EXPAND_SPLITS)
                if kind in ("q", "k"):
                    at = COL_Q if kind == "q" else COL_K
                    for k in range(KD):
                        c = slice(k * EXPAND_COLS + at, k * EXPAND_COLS + at + P)
                        ins = three(ring_bank(s), lambda h: WE[:, h, c], lambda h: XT[:, b, h, k], k == 0, k == KD - 1)
                    ins.then_inc(ring_full, 1)
                if kind == "loc":
                    for w in range(2):
                        for k in range(KD):
                            at = k * EXPAND_COLS + COL_LOC + (2 * i + w) * P
                            c = slice(at, at + P)
                            ins = three(ring_bank(s, w), lambda h: WE[:, h, c], lambda h: XT[:, b, h, k],
                                        k == 0, k == KD - 1)
                        ins.then_inc(ring_full, 1)
                if kind == "val":
                    t = slice(i * P, (i + 1) * P)
                    for k in range(KD):
                        c = slice(k * EXPAND_COLS + COL_VAL, k * EXPAND_COLS + COL_VAL + 2 * D)
                        ins = three(ring_bank(s), lambda h: XT[:, b, h, k, t], lambda h: WE[:, h, c],
                                    k == 0, k == KD - 1)
                    ins.then_inc(ring_full, 1)
                if kind == "score":
                    pe.wait_ge(qk_rows, 2 * b + 2)
                    w = (i + 1) * P
                    mm(acc_bank(s)[:, 0:w], QKS[:, 0, i * P:w], QKS[:, 1, 0:w], True, True).then_inc(acc_full, 1)
                if kind == "pt":
                    pe.wait_ge(probs_ready, SOFT[s] + 1)
                    for j in range(i + 1):
                        c = slice(j * P, (j + 1) * P)
                        ins = nc.tensor.transpose(ring_bank(s)[:, c], logits[:, i, c], ident)
                    ins.then_inc(ring_full, 1)
                if kind == "av":
                    pe.wait_ge(pt_lo, NT * (b + 1))
                    pe.wait_ge(gate_lo, GATES[("val", 0, b, NT - 1)] + 1)
                    c = slice(i * P, (i + 1) * P)
                    for j in range(NT):
                        ins = three(ring_bank(s)[:, j * P:S], lambda h: V[:, b, j, h, c],
                                    lambda h: PT[:, h, j, j * P:S], j == 0, j == NT - 1)
                    ins.then_inc(ring_full, 1)
                if kind == "out":
                    pe.wait_ge(av_lo, KD * (b + 1))
                    pe.wait_ge(gate_lo, GATES[("loc", 0, b, KD - 1)] + 1)
                    pe.wait_ge(att_split, N_EXPAND_SPLITS + N_PROJ_SPLITS)
                    t = slice(i * P, (i + 1) * P)
                    token_product(acc_bank(s), [lambda h, e=e: HID[:, NT * b + e, h, t] for e in range(EXP // P)],
                                  lambda e: WP[:, e].rearrange("p h d -> p (h d)")).then_inc(acc_full, 1)


def kernel(L0_attn_x, L0_attn_ln_gamma, L0_attn_ln_beta, L0_attn_expand, L0_attn_project, L0_attn_pos_mult,
           L0_ffn_W1, L0_ffn_W2, L0_ffn_W3):
    import numpy as np
    import concourse.bacc as bacc
    from concourse.bass_utils import run_bass_kernel_spmd

    x = np.ascontiguousarray(L0_attn_x)
    w13 = np.stack([np.asarray(L0_ffn_W1), np.asarray(L0_ffn_W3)]).reshape(2, NC, P, KD, P)
    w13 = np.ascontiguousarray(w13.transpose(1, 4, 0, 3, 2)).reshape(NC, P, 2 * KD * P)
    w2 = np.ascontiguousarray(np.asarray(L0_ffn_W2).reshape(D, NC, P).transpose(2, 1, 0)).reshape(P, NC * D)
    e = np.asarray(L0_attn_expand)
    q, k, lin, pre = e[:QK], e[QK:2 * QK], e[2 * QK:2 * QK + EXP], e[2 * QK + EXP:]
    local = [w[c * P:(c + 1) * P] for c in range(KD) for w in (pre, lin)]
    e = np.concatenate([q] * 4 + [k] * 4 + local + [pre[D:], lin[D:]])
    expand = np.ascontiguousarray(e.reshape(EXPAND_COLS, KD, P).transpose(2, 1, 0)).reshape(P, KD * EXPAND_COLS)
    proj = np.ascontiguousarray(np.asarray(L0_attn_project).reshape(D, EXP // P, P).transpose(2, 1, 0))
    proj = proj.reshape(P, EXP // P * D)
    gb = np.concatenate([np.asarray(L0_attn_ln_gamma).reshape(KD, P), np.asarray(L0_attn_ln_beta).reshape(KD, P)])
    gb = np.ascontiguousarray(gb.T)
    pos = np.asarray(L0_attn_pos_mult).reshape(1, 1)
    hadamard = np.ones((1, 1), np.float32)
    while len(hadamard) < P:
        hadamard = np.block([[hadamard, hadamard], [hadamard, -hadamard]])
    rows = np.arange(P)
    const = np.concatenate([np.eye(P), hadamard * (0.5 * H ** -0.5), -(rows // QK % 2)[:, None],
                            -(rows // (2 * QK))[:, None]], axis=1).astype(np.float32)

    nc = bacc.Bacc("TRN2", target_bir_lowering=False, num_devices=1)
    arrays = {"x": x, "w13": w13, "w2": w2, "expand": expand, "proj": proj, "const": const, "gamma_beta": gb,
              "pos_mult": pos}
    args = [nc.dram_tensor(f"{name}_in", a.shape, mybir.dt.from_np(a.dtype), kind="ExternalInput").ap()
            for name, a in arrays.items()]
    out = nc.dram_tensor("out", x.shape, F32, kind="ExternalOutput").ap()
    build_macaron(nc, *args, out)
    r = run_bass_kernel_spmd(nc, [{f"{name}_in": a for name, a in arrays.items()}], core_ids=[0])
    return r.results[0]["out"]
```

```python
from contextlib import ExitStack

import concourse.bass as bass
from concourse import mybir

P = 128
B, S, D, H = 2, 512, 256, 1024
QK, EXP = D // 8, 2 * D
NT = S // P
KD = D // P
NC = H // P
EPS = 1e-5
SCALE = float(QK) ** -0.5
MASKED = 3.0e38
HIDDEN_SLOTS = NC + 1
GATE_BUFS = 3
WARM_UP = 16
COL_Q, COL_K, COL_LOC, COL_VAL = 0, P, 2 * P, 2 * P + 4 * P
EXPAND_COLS = COL_VAL + 2 * D
SPLIT = 512
N_EXPAND_SPLITS = KD * EXPAND_COLS // SPLIT
N_PROJ_SPLITS = (EXP // P) * D // SPLIT

F32 = mybir.dt.float32
F32R = mybir.dt.float32r
ALU = mybir.AluOpType
ACT = mybir.ActivationFunctionType


def tiles(kind, n, b, count=NT):
    return [(kind, n, b, i) for i in range(count)]


def alternate(*lists):
    return [r[n] for n in range(max(map(len, lists))) for r in lists if n < len(r)]


def steps():
    order = tiles("t", 0, 0)
    for f in range(2):
        up = [tiles("up", f, b, NC) for b in range(B)]
        if f == 0:
            order += up[0][:4] + alternate(up[0][4:], tiles("t", 0, 1)) + tiles("had", 0, 0)
        else:
            order += up[0][:1] + tiles("out", 0, 1)[2:] + up[0][1:4] + alternate(tiles("t", 2, 1), up[0][4:])
        order += up[1][:1] + tiles("down", f, 0)
        if f == 1:
            order += up[1][1:] + tiles("down", f, 1)
            continue
        order += up[1][1:4] + alternate(tiles("t", 1, 0), up[1][4:])
        down, val = tiles("down", 0, 1), tiles("val", 0, 0)
        order += down[:1] + [("q", 0, 0, 0), ("k", 0, 0, 0)] + down[1:2] + [("loc", 0, 0, 0)] + tiles("score", 0, 0)
        order += down[2:] + [("loc", 0, 0, 1)] + val[:1] + alternate(val[1:], tiles("t", 1, 1))
        order += [("q", 0, 1, 0), ("k", 0, 1, 0)] + tiles("loc", 0, 1, KD) + tiles("score", 0, 1)
        order += tiles("val", 0, 1)[:2] + tiles("pt", 0, 0) + tiles("val", 0, 1)[2:] + tiles("av", 0, 0, KD)
        out, pt = tiles("out", 0, 0), tiles("pt", 0, 1)
        order += out[:1] + pt[:1] + out[1:2] + pt[1:2] + out[2:3] + pt[2:] + out[3:]
        order += tiles("av", 0, 1, KD) + tiles("t", 2, 0) + tiles("out", 0, 1)[:2]
    return order


STEPS = steps()
W2S_SPLITS_AFTER = {("up", 0, 0, 5): (0,), ("up", 0, 0, 6): (1, 2), ("up", 0, 0, 7): (3,)}
ATT_SPLITS_AFTER = {("down", 0, 0, 1): (0,), ("down", 0, 0, 2): (1, 2), ("down", 0, 0, 3): (3,),
                    ("up", 0, 1, 1): (4,), ("up", 0, 1, 2): (5,), ("up", 0, 1, 3): (6,)}


def deferred(s, following):
    if s[0] in ("up", "loc", "val"):
        return following[0] in ("up", "loc", "val") or following[:2] == ("t", 1)
    return s[:2] == ("t", 1) and (following[0] == "val" or following[:2] == ("t", 1))


def numbered(kinds):
    return {s: n for n, s in enumerate(s for s in STEPS if s[0] in kinds)}


GATES = numbered({"up", "loc", "val"})
NORMED = numbered({"t"})
ACCS = numbered({"t", "q", "k", "had", "down", "score", "pt", "out"})
SUMS = numbered({"down", "out"})
SOFT = numbered({"pt"})


def ring_places():
    at, places = 0, {}
    for s in STEPS:
        if s[0] in ("up", "loc"):
            places[s] = at
            at += 2
        elif s[0] in ("val", "av"):
            places[s] = at
            at += 1
    return places


RING = ring_places()


def banks_of(s):
    return 2 if s[0] in ("up", "loc") else 1


def ring_end(s):
    return RING[s] + banks_of(s)


def occupants(s):
    if s in ACCS:
        return [r for r in ACCS if ACCS[r] == ACCS[s] - 4]
    first = RING[s] - 4
    return [r for r in RING if RING[r] < first + banks_of(s) and ring_end(r) > max(first, 0)] if first + banks_of(s) > 0 else []


def cat_slot(b, e):
    return (NC - 1 if e == 0 else e - 1) if b == 0 else NT - 1 + e


def gate_slot(s):
    _, _, b, c = s
    return c if b == 0 else (NC if c == 0 else c - 1)


STATS = [("ffn0", 0), ("ffn0", 1), ("attention", 0), ("attention", 1), ("ffn1", 0), ("ffn1", 1)]


def stat(kind, b):
    return STATS.index((kind, b))


def build_macaron(nc, x_d, w13_d, w2_d, expand_d, proj_d, const_d, gb_d, pos_d, out_d):
    with ExitStack() as ctx:
        def sb(name, shape, dt=F32):
            return ctx.enter_context(nc.sbuf_tensor(name, shape, dt))

        def sem(name):
            return ctx.enter_context(nc.semaphore(name))

        X = sb("residual", [P, B, NT, D])
        raw = sb("w13_raw", [P, B * P * sum(range(1, NT + 1))])
        w13_raw = raw[:, 0:4 * 2 * KD * P].rearrange("p (r n) -> p r n", r=4)
        with nc.sbuf_tensor("w2_raw", [P, 2, NC * D], F32) as w2_raw:
            pass
        PT = sb("probs_T", [P, 2, NT, S], F32R)
        att_raw = w2_raw[:, :, :].rearrange("p a n -> p (a n)")
        W13 = sb("w13_split", [P, NC, 2, 2 * KD * P], F32R)
        W2 = sb("w2_split", [P, NC, 2, D], F32R)
        w2s = sb("w2_prod_split", [P, 2, NC * D], F32R)
        V = w2s[:, :, :].rearrange("p h (b t d) -> p b t h d", b=B, t=NT)
        WE = sb("expand_split", [P, 2, KD * EXPAND_COLS], F32R)
        WP = sb("proj_split", [P, EXP // P, 2, D], F32R)
        XT = sb("normed_T", [P, B, 2, KD, S], F32R)
        HID = sb("hidden_T", [P, HIDDEN_SLOTS, 2, S], F32R)
        QKS = sb("qk_rows", [P, 2, S], F32R)
        gated = sb("gated", [P, GATE_BUFS, S])
        outer = sb("outer_norm", [P, 2, D])
        normed = sb("normed", [P, NT, D])
        hfull = sb("affine_T", [P, 2, D])
        bias = sb("position_bias", [P, S])
        const = sb("const", [P, 2 * P + 2])
        ident, had = const[:, 0:P], const[:, P:2 * P]
        qmask, kmask = const[:, 2 * P:2 * P + 1], const[:, 2 * P + 1:2 * P + 2]
        HADR = sb("hadamard", [P, P], F32R)
        gb = sb("gamma_beta", [P, 2 * KD])
        warm = sb("warm", [P, S], mybir.dt.bfloat16)
        NS = len(STATS)
        bn = sb("bn", [P, NS * NT, 6])
        mv = sb("mean_var", [P, NS * NT, 2])
        ve = sb("var_eps", [P, NS * NT])
        rstd = sb("rstd", [P, NS * NT])
        inner = sb("inner_stats", [P, B, 4, NT])
        minus_half = sb("minus_half", [P, NT])
        pos = sb("pos", [P, 6])
        soft = sb("soft_stats", [P, B * NT, 3])

        ring = ctx.enter_context(nc.psum_tensor("ring", [P, 4, 512], F32))
        acc = ctx.enter_context(nc.psum_tensor("acc", [P, 4, 512], F32))

        x_in = [[sem(f"x_in{b}{t}") for t in range(NT)] for b in range(B)]
        w13_in = [sem(f"w13_in{c}") for c in range(NC)]
        w2_in, expand_in, proj_in = sem("w2_in"), sem("expand_in"), sem("proj_in")
        const_in, gb_in, pos_in, out_done = sem("const_in"), sem("gb_in"), sem("pos_in"), sem("out_done")
        ring_full, acc_full = sem("ring_full"), sem("acc_full")
        w13_hi, w13_split = sem("w13_hi"), sem("w13_split")
        w2_mixed, w2s_hi, w2s_split = sem("w2_mixed"), sem("w2s_hi"), sem("w2s_split")
        w2_hi, w2_lo, had_ready = sem("w2_hi"), sem("w2_lo"), sem("had_ready")
        att_hi, att_split = sem("att_hi"), sem("att_split")
        act_ready, gate_ready, gate_hi, gate_lo = sem("act_ready"), sem("gate_ready"), sem("gate_hi"), sem("gate_lo")
        bn_done, mv_done, var_ready, rstd_ready = sem("bn_done"), sem("mv_done"), sem("var_ready"), sem("rstd_ready")
        outer_ready, outer_added, normed_ready = sem("outer_ready"), sem("outer_added"), sem("normed_ready")
        inner_step = sem("inner_step")
        affine_ready, xt_hi, xt_lo = sem("affine_ready"), sem("xt_hi"), sem("xt_lo")
        x_done = sem("x_done")
        qk_hi, qk_rows = sem("qk_hi"), sem("qk_rows_ready")
        logits_ready, exp_ready, recip_ready, probs_ready = sem("logits_ready"), sem("exp_ready"), sem("recip_ready"), sem("probs_ready")
        pt_hi, pt_lo, av_hi, av_lo = sem("pt_hi"), sem("pt_lo"), sem("av_hi"), sem("av_lo")
        bias_ready, rel_ready, half_ready = sem("bias_ready"), sem("rel_ready"), sem("half_ready")
        warm_ready, table_ready = sem("warm_ready"), sem("table_ready")
        warm_done = sem("warm_done")
        pos_abs, pos_exp, pos_ln, pos_slope = sem("pos_abs"), sem("pos_exp"), sem("pos_ln"), sem("pos_slope")

        def logits(b, i):
            at = P * (b * sum(range(1, NT + 1)) + sum(range(1, i + 1)))
            return raw[:, at:at + (i + 1) * P]

        def ring_bank(s, n=0):
            return ring[:, (RING[s] + n) % 4]

        def acc_bank(s):
            return acc[:, ACCS[s] % 4]

        def filled(s):
            return (ring_full, ring_end(s)) if s in RING else (acc_full, ACCS[s] + 1)

        def gate_dst(s, part):
            kind, _, b, i = s
            if kind == "up":
                return HID[:, gate_slot(s), part, :]
            if kind == "loc":
                return HID[:, cat_slot(b, i), part, :]
            return V[:, b, i, part, :]

        def gate_width(s):
            return D if s[0] == "val" else S

        def gate_dst_free(eng, s):
            kind, f, b, i = s
            if kind == "up" and b == 1 and i > 0:
                eng.wait_ge(*filled(("down", f, 0, NT - 1)))
            elif kind == "up" and f == 1:
                held = [r for r in range(B) for e in range(EXP // P) if cat_slot(r, e) == gate_slot(s)]
                eng.wait_ge(*filled(("out", 0, held[0] if held else 0, NT - 1)))
            elif kind in ("loc",):
                eng.wait_ge(*filled(("down", 0, 0 if (b, i) == (0, 0) else 1, NT - 1)))
            elif kind == "val":
                eng.wait_ge(*filled(("had", 0, 0, 3)))

        def xt_free(eng, s):
            _, n, b, _ = s
            if n:
                last = ("up", 0, b, NC - 1) if n == 1 else ("val", 0, b, NT - 1)
                eng.wait_ge(*filled(last))

        def released_by(s):
            kind, f, b, i = s
            if kind in ("up", "loc", "val"):
                return gate_ready, GATES[s] + 1
            if kind == "t":
                return (affine_ready, KD * (NT * b + i + 1)) if f == 1 else (xt_lo, NORMED[s] + 1)
            if kind in ("q", "k"):
                return qk_rows, 2 * b + (1 if kind == "q" else 2)
            if kind == "pt":
                return pt_lo, SOFT[s] + 1
            if kind == "av":
                return av_lo, KD * b + i + 1
            if kind == "had":
                return w2_lo, i + 1
            if kind == "score":
                return logits_ready, NT * b + i + 1
            return x_done, SUMS[s] + 1

        block = ctx.enter_context(nc.Block())

        @block.sync
        def _(sp):
            def load_x(b, t):
                sp.dma_start(X[:, b, t], x_d[b, t * P:(t + 1) * P, :]).then_inc(x_in[b][t], 16)

            def load_w13(c):
                if c >= 4:
                    sp.wait_ge(w13_split, c - 3)
                sp.dma_start(w13_raw[:, c % 4], w13_d[c]).then_inc(w13_in[c], 16)

            for t in (0, 2):
                load_x(0, t)
            load_w13(0)
            load_w13(1)
            sp.dma_start(w2_raw[:, 0], w2_d).then_inc(w2_in, 16)
            load_w13(2)
            load_w13(3)
            for t in range(NT):
                load_x(1, t)
            for c in range(4, NC):
                load_w13(c)
            sp.wait_ge(w2s_split, 4)
            sp.dma_start(att_raw[:, 0:KD * EXPAND_COLS], expand_d).then_inc(expand_in, 16)
            sp.dma_start(att_raw[:, KD * EXPAND_COLS:KD * EXPAND_COLS + EXP // P * D], proj_d).then_inc(proj_in, 16)
            for b in range(B):
                for t in range(NT):
                    sp.wait_ge(x_done, NT * (4 + b) + t + 1)
                    sp.dma_start(out_d[b, t * P:(t + 1) * P, :], X[:, b, t]).then_inc(out_done, 16)
            sp.wait_ge(out_done, 16 * B * NT)

        @block.gpsimd
        def _(pool):
            nc.gpsimd.memset(minus_half[:], -0.5).then_inc(half_ready, 1)
            nc.gpsimd.memset(warm[:], 0.0).then_inc(warm_ready, 1)
            nc.gpsimd.iota(bias[:], pattern=[[-1, S]], base=S - P, channel_multiplier=1,
                           allow_small_or_imprecise_dtypes=True).then_inc(rel_ready, 1)
            pool.wait_ge(half_ready, 1)

            def columns(kind, b):
                return slice(stat(kind, b) * NT, (stat(kind, b) + 1) * NT)

            def reciprocal_roots(kind, b):
                c = columns(kind, b)
                pool.wait_ge(var_ready, stat(kind, b) + 1)
                nc.gpsimd.tensor_tensor(rstd[:, c], ve[:, c], minus_half[:], ALU.pow).then_inc(rstd_ready, 1)

            def inner_norm_scale(b):
                c, n = columns("attention", b), 5 * b
                var, var_eps, root, scale = (inner[:, b, m] for m in range(4))
                pool.wait_ge(rstd_ready, stat("attention", b) + 1)
                nc.gpsimd.tensor_tensor(var, mv[:, c, 1], rstd[:, c], ALU.mult).then_inc(inner_step, 1)
                pool.wait_ge(inner_step, n + 1)
                nc.gpsimd.tensor_tensor(var, var, rstd[:, c], ALU.mult).then_inc(inner_step, 1)
                pool.wait_ge(inner_step, n + 2)
                nc.gpsimd.tensor_scalar(var_eps, var, EPS, None, ALU.add).then_inc(inner_step, 1)
                pool.wait_ge(inner_step, n + 3)
                nc.gpsimd.tensor_tensor(root, var_eps, minus_half[:], ALU.pow).then_inc(inner_step, 1)
                pool.wait_ge(inner_step, n + 4)
                nc.gpsimd.tensor_tensor(scale, root, rstd[:, c], ALU.mult).then_inc(inner_step, 1)

            def add_outer(b):
                for t in range(NT):
                    n, c = NT * b + t, stat("attention", b) * NT + t
                    if n >= 2:
                        pool.wait_ge(outer_added, n - 1)
                    nc.gpsimd.tensor_scalar(outer[:, t % 2], X[:, b, t], mv[:, c, 0:1], rstd[:, c:c + 1],
                                            ALU.subtract, ALU.mult).then_inc(outer_ready, 1)
                    pool.wait_ge(outer_ready, n + 1)
                    pool.wait_ge(normed_ready, NORMED[("t", 1, b, t)] + 1)
                    nc.gpsimd.tensor_tensor(X[:, b, t], X[:, b, t], outer[:, t % 2], ALU.add).then_inc(outer_added, 1)

            reciprocal_roots("ffn0", 0)
            pool.wait_ge(w2_in, 16)
            for stage in range(3):
                h = 1 << stage
                src = w2_raw[:, stage % 2].rearrange("p (g two r) -> p g two r", two=2, r=h * D)
                dst = w2_raw[:, 1 - stage % 2].rearrange("p (g two r) -> p g two r", two=2, r=h * D)
                if stage:
                    pool.wait_ge(w2_mixed, 2 * stage)
                nc.gpsimd.tensor_tensor(dst[:, :, 0], src[:, :, 0], src[:, :, 1], ALU.add).then_inc(w2_mixed, 1)
                nc.gpsimd.tensor_tensor(dst[:, :, 1], src[:, :, 0], src[:, :, 1], ALU.subtract).then_inc(w2_mixed, 1)
                if stage == 1:
                    reciprocal_roots("ffn0", 1)
            pool.wait_ge(rel_ready, 1)
            pool.wait_ge(pos_slope, 3)
            nc.gpsimd.tensor_scalar(bias[:], bias[:], pos[:, 5:6], None, ALU.mult).then_inc(rel_ready, 1)
            pool.wait_ge(rel_ready, 2)
            nc.gpsimd.affine_select(out=bias[:], in_=bias[:], compare_op=ALU.is_ge, fill=MASKED,
                                    base=S - P, pattern=[[-1, S]], channel_multiplier=1).then_inc(bias_ready, 1)
            for b in range(B):
                reciprocal_roots("attention", b)
                inner_norm_scale(b)
                add_outer(b)
            reciprocal_roots("ffn1", 0)
            reciprocal_roots("ffn1", 1)

        @block.scalar
        def _(act):
            for t in (1, 3):
                act.dma_start(X[:, 0, t], x_d[0, t * P:(t + 1) * P, :]).then_inc(x_in[0][t], 16)
            act.dma_start(const[:], const_d).then_inc(const_in, 16)
            act.dma_start(gb[:], gb_d).then_inc(gb_in, 16)
            act.dma_start(pos[:, 0:1], pos_d.to_broadcast([P, 1])).then_inc(pos_in, 16)

            def split_w13(c):
                act.wait_ge(w13_in[c], 16)
                nc.scalar.activation(W13[:, c, 0], w13_raw[:, c % 4], ACT.Copy).then_inc(w13_hi, 1)

            def split_w2s(n):
                if n == 0:
                    act.wait_ge(w2_mixed, 6)
                r = slice(n * SPLIT, (n + 1) * SPLIT)
                nc.scalar.activation(w2s[:, 0, r], w2_raw[:, 1, r], ACT.Copy).then_inc(w2s_hi, 1)

            def split_att(n):
                act.wait_ge(expand_in if n < N_EXPAND_SPLITS else proj_in, 16)
                src = att_raw[:, n * SPLIT:(n + 1) * SPLIT]
                if n < N_EXPAND_SPLITS:
                    dst = WE[:, 0, n * SPLIT:(n + 1) * SPLIT]
                else:
                    m = n - N_EXPAND_SPLITS
                    dst = WP[:, 2 * m:2 * m + 2, 0, :]
                    src = src.rearrange("p (e d) -> p e d", d=D)
                nc.scalar.activation(dst, src, ACT.Copy).then_inc(att_hi, 1)

            def gate_activation(s):
                n, w = GATES[s], gate_width(s)
                act.wait_ge(ring_full, RING[s] + 1)
                if n >= GATE_BUFS:
                    act.wait_ge(gate_lo, n - GATE_BUFS + 1)
                nc.scalar.activation(gated[:, n % GATE_BUFS, 0:w], ring_bank(s)[:, 0:w],
                                     ACT.Silu if s[0] == "up" else ACT.Gelu).then_inc(act_ready, 1)

            def gate_high(s):
                n = GATES[s]
                act.wait_ge(gate_ready, n + 1)
                gate_dst_free(act, s)
                nc.scalar.activation(gate_dst(s, 0), gated[:, n % GATE_BUFS, 0:gate_width(s)], ACT.Copy)\
                    .then_inc(gate_hi, 1)

            def position_slope():
                act.wait_ge(pos_abs, 2)
                nc.scalar.activation(pos[:, 2:3], pos[:, 1:2], ACT.Exp, scale=-1.0).then_inc(pos_exp, 1)
                act.wait_ge(pos_exp, 1)
                nc.scalar.activation(pos[:, 3:4], pos[:, 2:3], ACT.Ln, bias=1.0).then_inc(pos_ln, 1)

            def exponentials(b):
                for i in range(NT):
                    n = NT * b + i
                    act.wait_ge(logits_ready, n + 1)
                    row = logits(b, i)
                    nc.scalar.activation(row, row, ACT.Exp, scale=-1.0, bias=soft[:, n, 0:1],
                                         accum_out=soft[:, n, 1:2]).then_inc(exp_ready, 1)

            def transposed_high(s):
                _, f, b, i = s
                xt_free(act, s)
                if f == 1:
                    a = NT * b + i
                    act.wait_ge(affine_ready, KD * (a + 1))
                    src = hfull[:, a % 2]
                else:
                    act.wait_ge(*filled(s))
                    src = acc_bank(s)[:, 0:D]
                nc.scalar.activation(XT[:, b, 0, :, i * P:(i + 1) * P], src.rearrange("p (k m) -> p k m", k=KD),
                                     ACT.Copy).then_inc(xt_hi, 1)

            act.wait_ge(half_ready, 1)
            nc.scalar.activation(pos[:, 5:6], minus_half[:, 0:1], ACT.Silu).then_inc(table_ready, 1)
            split_w13(0)
            pending = None
            for s in STEPS:
                kind, f, b, i = s
                if pending and not deferred(pending, s):
                    gate_high(pending)
                    pending = None
                if kind in ("up", "loc", "val"):
                    gate_activation(s)
                if pending:
                    gate_high(pending)
                pending = s if kind in ("up", "loc", "val") else None
                if s == ("t", 0, 0, NT - 1):
                    split_w13(1)
                if (kind, f, b) == ("up", 0, 0) and i + 2 < NC:
                    split_w13(i + 2)
                if s == ("up", 0, 0, 2):
                    nc.scalar.activation(HADR[:], had, ACT.Copy).then_inc(had_ready, 1)
                for n in W2S_SPLITS_AFTER.get(s, ()):
                    split_w2s(n)
                for n in ATT_SPLITS_AFTER.get(s, ()):
                    split_att(n)
                if kind == "t":
                    transposed_high(s)
                if kind == "had":
                    act.wait_ge(*filled(s))
                    nc.scalar.activation(W2[:, 2 * i:2 * i + 2, 0, :],
                                         acc_bank(s).rearrange("p (c d) -> p c d", d=D), ACT.Copy).then_inc(w2_hi, 1)
                if kind in ("q", "k"):
                    act.wait_ge(*filled(s))
                    if b:
                        act.wait_ge(*filled(("score", 0, 0, NT - 1)))
                    which = 0 if kind == "q" else 1
                    nc.scalar.activation(QKS[:, which], acc_bank(s), ACT.Copy,
                                         scale=-1.0 if kind == "q" else 1.0).then_inc(qk_hi, 1)
                if kind == "pt":
                    act.wait_ge(*filled(s))
                    if b:
                        act.wait_ge(*filled(("av", 0, 0, KD - 1)))
                    nc.scalar.activation(PT[:, 0, 0:i + 1, i * P:(i + 1) * P],
                                         acc_bank(s)[:, 0:(i + 1) * P].rearrange("p (j q) -> p j q", q=P),
                                         ACT.Copy).then_inc(pt_hi, 1)
                if kind == "av":
                    act.wait_ge(*filled(s))
                    nc.scalar.activation(HID[:, cat_slot(b, KD + i), 0, :], ring_bank(s), ACT.Copy).then_inc(av_hi, 1)
                if s == ("down", 0, 0, 0):
                    position_slope()
                if s == ("loc", 0, 1, KD - 1):
                    gate_high(s)
                    pending = None
                    exponentials(0)
                if s == ("score", 0, 1, NT - 1):
                    exponentials(1)

        @block.vector
        def _(dve):
            def split_w13(c):
                dve.wait_ge(w13_hi, c + 1)
                nc.vector.tensor_tensor(W13[:, c, 1], w13_raw[:, c % 4], W13[:, c, 0].bitcast(F32),
                                        ALU.subtract).then_inc(w13_split, 1)

            def split_w2s(n):
                dve.wait_ge(w2s_hi, n + 1)
                r = slice(n * SPLIT, (n + 1) * SPLIT)
                nc.vector.tensor_tensor(w2s[:, 1, r], w2_raw[:, 1, r], w2s[:, 0, r].bitcast(F32),
                                        ALU.subtract).then_inc(w2s_split, 1)

            def split_att(n):
                dve.wait_ge(att_hi, n + 1)
                src = att_raw[:, n * SPLIT:(n + 1) * SPLIT]
                if n < N_EXPAND_SPLITS:
                    hi, lo = (WE[:, h, n * SPLIT:(n + 1) * SPLIT] for h in range(2))
                else:
                    m = n - N_EXPAND_SPLITS
                    hi, lo = (WP[:, 2 * m:2 * m + 2, h, :] for h in range(2))
                    src = src.rearrange("p (e d) -> p e d", d=D)
                nc.vector.tensor_tensor(lo, src, hi.bitcast(F32), ALU.subtract).then_inc(att_split, 1)

            def statistics(kind, b):
                first = stat(kind, b) * NT
                for t in range(NT):
                    if kind == "ffn0":
                        dve.wait_ge(x_in[b][t], 16)
                    nc.vector.bn_stats(bn[:, first + t], X[:, b, t]).then_inc(bn_done, 1)
                for t in range(NT):
                    dve.wait_ge(bn_done, first + t + 1)
                    nc.vector.bn_aggr(mv[:, first + t], bn[:, first + t]).then_inc(mv_done, 1)
                dve.wait_ge(mv_done, first + NT)
                nc.vector.tensor_scalar(ve[:, first:first + NT], mv[:, first:first + NT, 1], EPS, None, ALU.add)\
                    .then_inc(var_ready, 1)

            def normalize(kind, b, s):
                t = s[3]
                n = stat(kind, b) * NT + t
                normed_free(s)
                scale = inner[:, b, 3, t:t + 1] if kind == "attention" else rstd[:, n:n + 1]
                nc.vector.tensor_scalar(normed[:, t], X[:, b, t], mv[:, n, 0:1], scale, ALU.subtract, ALU.mult)\
                    .then_inc(normed_ready, 1)

            def normed_free(s):
                n = NORMED[s]
                if n >= NT:
                    before = next(r for r in NORMED if NORMED[r] == n - NT)
                    dve.wait_ge(*filled(before))

            def ffn_statistics(f, b):
                if f:
                    dve.wait_ge(x_done, SUMS[("out", 0, b, NT - 1)] + 1)
                statistics(f"ffn{f}", b)

            def ffn_normalize(f, b):
                dve.wait_ge(rstd_ready, stat(f"ffn{f}", b) + 1)
                for t in range(NT):
                    normalize(f"ffn{f}", b, ("t", 2 * f, b, t))

            def attention_statistics(b):
                dve.wait_ge(x_done, SUMS[("down", 0, b, NT - 1)] + 1)
                statistics("attention", b)

            def attention_normalize(b):
                dve.wait_ge(inner_step, 5 * (b + 1))
                for t in range(NT):
                    normalize("attention", b, ("t", 1, b, t))

            def position_magnitude():
                dve.wait_ge(pos_in, 16)
                nc.vector.tensor_scalar(pos[:, 4:5], pos[:, 0:1], -1.0, None, ALU.mult).then_inc(pos_abs, 1)
                dve.wait_ge(pos_abs, 1)
                nc.vector.tensor_tensor(pos[:, 1:2], pos[:, 0:1], pos[:, 4:5], ALU.max).then_inc(pos_abs, 1)

            def position_slope():
                dve.wait_ge(pos_ln, 1)
                nc.vector.tensor_scalar(pos[:, 4:5], pos[:, 0:1], 0.0, None, ALU.max).then_inc(pos_slope, 1)
                dve.wait_ge(pos_slope, 1)
                nc.vector.tensor_tensor(pos[:, 5:6], pos[:, 4:5], pos[:, 3:4], ALU.add).then_inc(pos_slope, 1)
                dve.wait_ge(pos_slope, 2)
                nc.vector.tensor_scalar(pos[:, 5:6], pos[:, 5:6], 1.0 / SCALE, None, ALU.mult).then_inc(pos_slope, 1)

            def gate(s):
                n, w = GATES[s], gate_width(s)
                linear = ring_bank(s)[:, D:2 * D] if s[0] == "val" else ring_bank(s, 1)
                tile = gated[:, n % GATE_BUFS, 0:w]
                dve.wait_ge(act_ready, n + 1)
                dve.wait_ge(*filled(s))
                nc.vector.tensor_tensor(tile, tile, linear, ALU.mult).then_inc(gate_ready, 1)

            def gate_low(s):
                n = GATES[s]
                tile = gated[:, n % GATE_BUFS, 0:gate_width(s)]
                dve.wait_ge(gate_hi, n + 1)
                nc.vector.tensor_tensor(gate_dst(s, 1), tile, gate_dst(s, 0).bitcast(F32), ALU.subtract)\
                    .then_inc(gate_lo, 1)

            def affine(s):
                _, _, b, i = s
                n, a = NORMED[s], NT * b + i
                dve.wait_ge(*filled(s))
                if a >= 2:
                    dve.wait_ge(xt_lo, n - 1)
                for k in range(KD):
                    c = slice(k * P, (k + 1) * P)
                    nc.vector.tensor_scalar(hfull[:, a % 2, c], acc_bank(s)[:, c], gb[:, k:k + 1],
                                            gb[:, KD + k:KD + k + 1], ALU.mult, ALU.add).then_inc(affine_ready, 1)

            def transposed_low(s):
                _, f, b, i = s
                n = NORMED[s]
                if f == 1:
                    source = hfull[:, (NT * b + i) % 2]
                    dve.wait_ge(affine_ready, KD * (NT * b + i + 1))
                else:
                    source = acc_bank(s)[:, 0:D]
                dve.wait_ge(xt_hi, n + 1)
                c = slice(i * P, (i + 1) * P)
                nc.vector.tensor_tensor(XT[:, b, 1, :, c], source.rearrange("p (k m) -> p k m", k=KD),
                                        XT[:, b, 0, :, c].bitcast(F32), ALU.subtract).then_inc(xt_lo, 1)

            def qk_low(s):
                kind, _, b, _ = s
                n = 2 * b + (kind == "k")
                part, mask = QKS[:, n % 2], (qmask, kmask)[n % 2]
                dve.wait_ge(qk_hi, n + 1)
                nc.vector.scalar_tensor_tensor(part, part.bitcast(F32), mask, acc_bank(s), ALU.mult,
                                               ALU.subtract if kind == "q" else ALU.add).then_inc(qk_rows, 1)

            def negated_logits(s):
                _, _, b, i = s
                w = (i + 1) * P
                dve.wait_ge(*filled(s))
                if b == 0 and i == 0:
                    dve.wait_ge(bias_ready, 1)
                    dve.wait_ge(w13_split, NC)
                nc.vector.tensor_tensor_reduce(out=logits(b, i), in0=acc_bank(s)[:, 0:w],
                                               in1=bias[:, S - w:S], scale=SCALE, scalar=MASKED, op0=ALU.add,
                                               op1=ALU.min, accum_out=soft[:, NT * b + i, 0:1]).then_inc(logits_ready, 1)

            def probabilities(b, i):
                n = NT * b + i
                row = logits(b, i)
                dve.wait_ge(exp_ready, n + 1)
                nc.vector.reciprocal(soft[:, n, 2:3], soft[:, n, 1:2]).then_inc(recip_ready, 1)
                dve.wait_ge(recip_ready, n + 1)
                nc.vector.tensor_scalar(row, row, soft[:, n, 2:3], None, ALU.mult).then_inc(probs_ready, 1)

            def add_product(s):
                kind, _, b, t = s
                dve.wait_ge(*filled(s))
                if kind == "out":
                    dve.wait_ge(outer_added, NT * b + t + 1)
                nc.vector.tensor_tensor(X[:, b, t], X[:, b, t], acc_bank(s)[:, 0:D], ALU.add).then_inc(x_done, 1)

            ffn_statistics(0, 0)
            ffn_normalize(0, 0)

            def low_part(s):
                (transposed_low if s[0] == "t" else gate_low)(s)

            pending = None
            for s in STEPS:
                kind, f, b, i = s
                if pending and not deferred(pending, s):
                    low_part(pending)
                    pending = None
                if kind in ("up", "loc", "val"):
                    gate(s)
                if kind == "t" and f == 1:
                    if s == ("t", 1, 0, 0):
                        dve.wait_ge(gb_in, 16)
                    affine(s)
                if pending:
                    low_part(pending)
                pending = s if kind in ("up", "loc", "val") or (kind, f) == ("t", 1) else None
                if s == ("t", 0, 0, 0):
                    split_w13(0)
                if (kind, f, b) == ("up", 0, 0) and i + 2 < NC:
                    split_w13(i + 2)
                if s == ("up", 0, 0, 1):
                    ffn_statistics(0, 1)
                if s == ("up", 0, 0, 2):
                    position_magnitude()
                if s == ("up", 0, 0, 3):
                    ffn_normalize(0, 1)
                for n in W2S_SPLITS_AFTER.get(s, ()):
                    split_w2s(n)
                if kind == "t" and f != 1:
                    transposed_low(s)
                    if s == ("t", 0, 0, NT - 1):
                        split_w13(1)
                if kind == "had":
                    dve.wait_ge(w2_hi, i + 1)
                    nc.vector.tensor_tensor(W2[:, 2 * i:2 * i + 2, 1, :],
                                            acc_bank(s).rearrange("p (c d) -> p c d", d=D),
                                            W2[:, 2 * i:2 * i + 2, 0, :].bitcast(F32), ALU.subtract).then_inc(w2_lo, 1)
                for n in ATT_SPLITS_AFTER.get(s, ()):
                    split_att(n)
                if kind in ("down", "out"):
                    add_product(s)
                if kind in ("q", "k"):
                    qk_low(s)
                if kind == "score":
                    negated_logits(s)
                if kind == "pt":
                    dve.wait_ge(pt_hi, SOFT[s] + 1)
                    high, low = (PT[:, h, 0:i + 1, i * P:(i + 1) * P] for h in range(2))
                    nc.vector.tensor_tensor(low, acc_bank(s)[:, 0:(i + 1) * P].rearrange("p (j q) -> p j q", q=P),
                                            high.bitcast(F32), ALU.subtract).then_inc(pt_lo, 1)
                if kind == "av":
                    dve.wait_ge(av_hi, KD * b + i + 1)
                    high, low = (HID[:, cat_slot(b, KD + i), h, :] for h in range(2))
                    nc.vector.tensor_tensor(low, ring_bank(s), high.bitcast(F32), ALU.subtract).then_inc(av_lo, 1)
                if s == ("down", 0, 0, NT - 1):
                    attention_statistics(0)
                if s == ("up", 0, 1, 2):
                    attention_normalize(0)
                if s == ("down", 0, 0, 1):
                    position_slope()
                if s == ("down", 0, 1, NT - 1):
                    attention_statistics(1)
                if s == ("loc", 0, 0, 1):
                    attention_normalize(1)
                if s == ("av", 0, 0, KD - 1):
                    for t in range(NT):
                        probabilities(1, t)
                if s == ("out", 0, 0, NT - 1):
                    ffn_statistics(1, 0)
                if s == ("av", 0, 1, 0):
                    ffn_normalize(1, 0)
                if s == ("out", 0, 1, NT - 1):
                    ffn_statistics(1, 1)
                if s == ("up", 1, 0, 2):
                    ffn_normalize(1, 1)
                if s == ("score", 0, 1, NT - 1):
                    for t in range(NT):
                        probabilities(0, t)

        @block.tensor
        def _(pe):
            def mm(out, stationary, moving, start, stop):
                return nc.tensor.matmul(out, stationary, moving, start=start, stop=stop)

            def three(out, stationary, moving, start, stop):
                mm(out, stationary(0), moving(0), start, False)
                mm(out, stationary(0), moving(1), False, False)
                return mm(out, stationary(1), moving(0), False, stop)

            def bank_free(s):
                for r in occupants(s):
                    pe.wait_ge(*released_by(r))

            pe.wait_ge(warm_ready, 1)
            for _ in range(WARM_UP):
                ins = mm(ring[:, 3], warm[:, 0:P], warm[:], True, True)
            ins.then_inc(warm_done, 1)
            pe.wait_ge(warm_done, 1)
            for s in STEPS:
                kind, f, b, i = s
                bank_free(s)
                if kind == "t":
                    if s == ("t", 0, 0, 0):
                        pe.wait_ge(const_in, 16)
                    pe.wait_ge(normed_ready, NORMED[s] + 1)
                    for k in range(KD):
                        c = slice(k * P, (k + 1) * P)
                        ins = nc.tensor.transpose(acc_bank(s)[:, c], normed[:, i, c], ident)
                    ins.then_inc(acc_full, 1)
                if kind == "up":
                    pe.wait_ge(xt_lo, NORMED[("t", 2 * f, b, NT - 1)] + 1)
                    pe.wait_ge(w13_split, i + 1)
                    for w in range(2):
                        for k in range(KD):
                            c = slice((w * KD + k) * P, (w * KD + k + 1) * P)
                            ins = three(ring_bank(s, w), lambda h: W13[:, i, h, c], lambda h: XT[:, b, h, k],
                                        k == 0, k == KD - 1)
                        ins.then_inc(ring_full, 1)
                if kind == "had":
                    pe.wait_ge(had_ready, 1)
                    pe.wait_ge(w2s_split, i + 1)
                    r = slice(i * SPLIT, (i + 1) * SPLIT)
                    mm(acc_bank(s), HADR[:], w2s[:, 0, r], True, False)
                    mm(acc_bank(s), HADR[:], w2s[:, 1, r], False, True).then_inc(acc_full, 1)
                if kind == "down":
                    t = slice(i * P, (i + 1) * P)
                    for c in range(NC):
                        if (f, b, i) == (0, 0, 0) and c % 2 == 0:
                            pe.wait_ge(w2_lo, c // 2 + 1)
                        if i == 0:
                            pe.wait_ge(gate_lo, GATES[("up", f, b, c)] + 1)
                        slot = gate_slot(("up", f, b, c))
                        ins = three(acc_bank(s)[:, 0:D], lambda h: HID[:, slot, h, t], lambda h: W2[:, c, h],
                                    c == 0, c == NC - 1)
                    ins.then_inc(acc_full, 1)
                if kind in ("q", "k", "loc", "val"):
                    pe.wait_ge(xt_lo, NORMED[("t", 1, b, NT - 1)] + 1)
                    pe.wait_ge(att_split, N_EXPAND_SPLITS)
                if kind in ("q", "k"):
                    at = COL_Q if kind == "q" else COL_K
                    for k in range(KD):
                        c = slice(k * EXPAND_COLS + at, k * EXPAND_COLS + at + P)
                        ins = three(acc_bank(s), lambda h: WE[:, h, c], lambda h: XT[:, b, h, k], k == 0, k == KD - 1)
                    ins.then_inc(acc_full, 1)
                if kind == "loc":
                    for w in range(2):
                        for k in range(KD):
                            at = k * EXPAND_COLS + COL_LOC + (2 * i + w) * P
                            c = slice(at, at + P)
                            ins = three(ring_bank(s, w), lambda h: WE[:, h, c], lambda h: XT[:, b, h, k],
                                        k == 0, k == KD - 1)
                        ins.then_inc(ring_full, 1)
                if kind == "val":
                    t = slice(i * P, (i + 1) * P)
                    for k in range(KD):
                        c = slice(k * EXPAND_COLS + COL_VAL, k * EXPAND_COLS + COL_VAL + 2 * D)
                        ins = three(ring_bank(s), lambda h: XT[:, b, h, k, t], lambda h: WE[:, h, c],
                                    k == 0, k == KD - 1)
                    ins.then_inc(ring_full, 1)
                if kind == "score":
                    pe.wait_ge(qk_rows, 2 * b + 2)
                    w = (i + 1) * P
                    mm(acc_bank(s)[:, 0:w], QKS[:, 0, i * P:w], QKS[:, 1, 0:w], True, True).then_inc(acc_full, 1)
                if kind == "pt":
                    pe.wait_ge(probs_ready, SOFT[s] + 1)
                    for j in range(i + 1):
                        c = slice(j * P, (j + 1) * P)
                        ins = nc.tensor.transpose(acc_bank(s)[:, c], logits(b, i)[:, c], ident)
                    ins.then_inc(acc_full, 1)
                if kind == "av":
                    pe.wait_ge(pt_lo, NT * (b + 1))
                    pe.wait_ge(gate_lo, GATES[("val", 0, b, NT - 1)] + 1)
                    c = slice(i * P, (i + 1) * P)
                    for j in range(NT):
                        ins = three(ring_bank(s)[:, j * P:S], lambda h: V[:, b, j, h, c],
                                    lambda h: PT[:, h, j, j * P:S], j == 0, j == NT - 1)
                    ins.then_inc(ring_full, 1)
                if kind == "out":
                    t = slice(i * P, (i + 1) * P)
                    for e in range(EXP // P):
                        if i == 0 and e == 0:
                            pe.wait_ge(gate_lo, GATES[("loc", 0, b, KD - 1)] + 1)
                            pe.wait_ge(att_split, N_EXPAND_SPLITS + N_PROJ_SPLITS)
                        if i == 0 and e >= KD:
                            pe.wait_ge(av_lo, KD * b + e - KD + 1)
                        ins = three(acc_bank(s)[:, 0:D], lambda h: HID[:, cat_slot(b, e), h, t], lambda h: WP[:, e, h],
                                    e == 0, e == EXP // P - 1)
                    ins.then_inc(acc_full, 1)


def kernel(L0_attn_x, L0_attn_ln_gamma, L0_attn_ln_beta, L0_attn_expand, L0_attn_project, L0_attn_pos_mult,
           L0_ffn_W1, L0_ffn_W2, L0_ffn_W3):
    import numpy as np
    import concourse.bacc as bacc
    from concourse.bass_utils import run_bass_kernel_spmd

    x = np.ascontiguousarray(L0_attn_x)
    w13 = np.stack([np.asarray(L0_ffn_W1), np.asarray(L0_ffn_W3)]).reshape(2, NC, P, KD, P)
    w13 = np.ascontiguousarray(w13.transpose(1, 4, 0, 3, 2)).reshape(NC, P, 2 * KD * P)
    w2 = np.ascontiguousarray(np.asarray(L0_ffn_W2).reshape(D, NC, P).transpose(2, 1, 0)).reshape(P, NC * D)
    e = np.asarray(L0_attn_expand)
    q, k, lin, pre = e[:QK], e[QK:2 * QK], e[2 * QK:2 * QK + EXP], e[2 * QK + EXP:]
    local = [w[c * P:(c + 1) * P] for c in range(KD) for w in (pre, lin)]
    e = np.concatenate([q] * 4 + [k] * 4 + local + [pre[D:], lin[D:]])
    expand = np.ascontiguousarray(e.reshape(EXPAND_COLS, KD, P).transpose(2, 1, 0)).reshape(P, KD * EXPAND_COLS)
    proj = np.ascontiguousarray(np.asarray(L0_attn_project).reshape(D, EXP // P, P).transpose(2, 1, 0))
    proj = proj.reshape(P, EXP // P * D)
    gb = np.concatenate([np.asarray(L0_attn_ln_gamma).reshape(KD, P), np.asarray(L0_attn_ln_beta).reshape(KD, P)])
    gb = np.ascontiguousarray(gb.T)
    pos = np.asarray(L0_attn_pos_mult).reshape(1, 1)
    hadamard = np.ones((1, 1), np.float32)
    while len(hadamard) < P:
        hadamard = np.block([[hadamard, hadamard], [hadamard, -hadamard]])
    rows = np.arange(P)
    const = np.concatenate([np.eye(P), hadamard * (0.5 * H ** -0.5), -(rows // QK % 2)[:, None],
                            -(rows // (2 * QK))[:, None]], axis=1).astype(np.float32)

    nc = bacc.Bacc("TRN2", target_bir_lowering=False, num_devices=1)
    arrays = {"x": x, "w13": w13, "w2": w2, "expand": expand, "proj": proj, "const": const, "gamma_beta": gb,
              "pos_mult": pos}
    args = [nc.dram_tensor(f"{name}_in", a.shape, mybir.dt.from_np(a.dtype), kind="ExternalInput").ap()
            for name, a in arrays.items()]
    out = nc.dram_tensor("out", x.shape, F32, kind="ExternalOutput").ap()
    build_macaron(nc, *args, out)
    r = run_bass_kernel_spmd(nc, [{f"{name}_in": a for name, a in arrays.items()}], core_ids=[0])
    return r.results[0]["out"]
```

```python
from contextlib import ExitStack

import concourse.bass as bass
from concourse import mybir

P = 128
B, S, D, H = 2, 512, 256, 1024
QK, EXP = D // 8, 2 * D
NT = S // P
KD = D // P
NC = H // P
EPS = 1e-5
SCALE = float(QK) ** -0.5
MASKED = 3.0e38
HIDDEN_SLOTS = NC + 1
GATE_BUFS = 3
POOL_W13_SPLITS = 2
WARM_UP, WARM_UP_AFTER_T = 10, 2
COL_QK, COL_LOC, COL_VAL = 0, P, P + 4 * P
EXPAND_COLS = COL_VAL + 2 * D
SPLIT = 512
N_EXPAND_SPLITS = -(-KD * EXPAND_COLS // SPLIT)
N_PROJ_SPLITS = (EXP // P) * D // SPLIT

F32 = mybir.dt.float32
F32R = mybir.dt.float32r
ALU = mybir.AluOpType
ACT = mybir.ActivationFunctionType


def tiles(kind, n, b, count=NT):
    return [(kind, n, b, i) for i in range(count)]


def alternate(*lists):
    return [r[n] for n in range(max(map(len, lists))) for r in lists if n < len(r)]


def steps():
    def first_ffn():
        up, t = [tiles("up", 0, b, NC) for b in range(B)], [tiles("t", n, 1 - n) for n in range(B)]
        return (tiles("t", 0, 0) + up[0][:6] + t[0][:2] + up[0][6:7] + t[0][2:] + up[0][7:] + tiles("had", 0, 0)
                + up[1][:1] + tiles("down", 0, 0) + up[1][1:4] + alternate(t[1], up[1][4:]))

    def attention():
        down, t = tiles("down", 0, 1), tiles("t", 1, 1)
        loc, val, score, pt, av = ([tiles(kind, 0, b, n) for b in range(B)] for kind, n in
                                   (("loc", KD), ("val", NT), ("score", NT), ("pt", NT), ("av", KD)))
        return ([("qk", 0, 0, 0)] + down[:3] + score[0] + down[3:]
                + loc[0] + t + val[0][:3] + [("qk", 0, 1, 0)] + val[0][3:] + pt[0]
                + loc[1][:1] + av[0][:1] + score[1] + av[0][1:] + loc[1][1:] + pt[1] + val[1])

    def outputs():
        head, tail, t = tiles("open", 0, 1), tiles("out", 0, 1), tiles("t", 2, 0)
        return (alternate(tiles("open", 0, 0), tiles("out", 0, 0)) + tiles("av", 0, 1, KD)
                + head[:2] + t[:1] + tail[:1] + t[1:2] + tail[1:2] + head[2:3] + t[2:3] + tail[2:3] + t[3:]
                + head[3:] + tail[3:])

    def second_ffn():
        up = [tiles("up", 1, b, NC) for b in range(B)]
        return (up[0][:4] + alternate(tiles("t", 2, 1), up[0][4:]) + up[1][:1] + tiles("down", 1, 0)
                + up[1][1:] + tiles("down", 1, 1))

    return first_ffn() + attention() + outputs() + second_ffn()


STEPS = steps()
W2S_SPLITS_AFTER = {("up", 0, 0, 5): (0, 1), ("up", 0, 0, 6): (2, 3)}
ATT_SPLITS_AFTER = {("down", 0, 0, 1): (0,), ("down", 0, 0, 2): (1, 2), ("down", 0, 0, 3): (3,),
                    ("up", 0, 1, 1): (4,), ("up", 0, 1, 2): (5,), ("up", 0, 1, 3): (6,)}
QK_ROWS_AFTER = {("down", 0, 1, 0): 0, ("pt", 0, 0, NT - 1): 1}


def deferred(following):
    return following[0] in ("up", "loc", "val", "t")


def numbered(kinds):
    return {s: n for n, s in enumerate(s for s in STEPS if s[0] in kinds)}


GATES = numbered({"up", "loc", "val"})
NORMED = numbered({"t"})
ACCS = numbered({"t", "qk", "had", "down", "score", "pt", "out"})
ACC_PLACES = {("out",) + s[1:] if s[0] == "open" else s: n
              for s, n in numbered({"t", "qk", "had", "down", "score", "pt", "open"}).items()}
SUMS = numbered({"down", "out"})
SOFT = numbered({"pt"})


def ring_places():
    at, places = 0, {}
    for s in STEPS:
        if s[0] in ("up", "loc"):
            places[s] = at
            at += 2
        elif s[0] in ("val", "av"):
            places[s] = at
            at += 1
    return places


RING = ring_places()


def banks_of(s):
    return 2 if s[0] in ("up", "loc") else 1


def ring_end(s):
    return RING[s] + banks_of(s)


def occupants(s):
    if s in ACC_PLACES:
        return [r for r in ACC_PLACES if ACC_PLACES[r] == ACC_PLACES[s] - 4]
    first = RING[s] - 4
    return [r for r in RING if RING[r] < first + banks_of(s) and ring_end(r) > first]


def split_columns(n):
    if n < N_EXPAND_SPLITS:
        return slice(n * SPLIT, min((n + 1) * SPLIT, KD * EXPAND_COLS))
    first = KD * EXPAND_COLS + (n - N_EXPAND_SPLITS) * SPLIT
    return slice(first, first + SPLIT)


def cat_slot(b, e):
    return (NC - 1 if e == 0 else e - 1) if b == 0 else NT - 1 + e


def gate_slot(s):
    _, _, b, c = s
    return c if b == 0 else (NC if c == 0 else c - 1)


STATS = [("ffn0", 0), ("ffn0", 1), ("attention", 0), ("attention", 1), ("ffn1", 0), ("ffn1", 1)]


def stat(kind, b):
    return STATS.index((kind, b))


def roots_made(kind, b):
    return stat(kind, b) + 2


def build_macaron(nc, x_d, w13_d, w2_d, expand_d, proj_d, const_d, gb_d, pos_d, out_d):
    with ExitStack() as ctx:
        def sb(name, shape, dt=F32):
            return ctx.enter_context(nc.sbuf_tensor(name, shape, dt))

        def sem(name):
            return ctx.enter_context(nc.semaphore(name))

        X = sb("residual", [P, B, NT, D])
        raw = sb("w13_raw", [P, B * P * sum(range(1, NT + 1))])
        w13_raw = raw[:, 0:4 * 2 * KD * P].rearrange("p (r n) -> p r n", r=4)
        with nc.sbuf_tensor("w2_raw", [P, 2, NC * D], F32) as w2_raw:
            pass
        PT = sb("probs_T", [P, 2, NT, S], F32R)
        att_raw = w2_raw[:, :, :].rearrange("p a n -> p (a n)")
        W13 = sb("w13_split", [P, NC, 2, 2 * KD * P], F32R)
        W2 = sb("w2_split", [P, NC, 2, D], F32R)
        w2s = sb("w2_prod_split", [P, 2, NC * D], F32R)
        V = w2s[:, :, :].rearrange("p h (b t d) -> p b t h d", b=B, t=NT)
        WE = sb("expand_split", [P, 2, KD * EXPAND_COLS], F32R)
        WP = sb("proj_split", [P, EXP // P, 2, D], F32R)
        XT = sb("normed_T", [P, B, 2, KD, S], F32R)
        HID = sb("hidden_T", [P, HIDDEN_SLOTS, 2, S], F32R)
        QKS = sb("qk_rows", [P, 2, S], F32R)
        gated = sb("gated", [P, GATE_BUFS, S])
        outer = sb("outer_norm", [P, 2, D])
        normed = sb("normed", [P, NT, D])
        hfull = sb("affine_T", [P, 2, D])
        bias = sb("position_bias", [P, S])
        const = sb("const", [P, 2 * P + 2])
        ident, had = const[:, 0:P], const[:, P:2 * P]
        qmask, kmask = const[:, 2 * P:2 * P + 1], const[:, 2 * P + 1:2 * P + 2]
        HADR = sb("hadamard", [P, P], F32R)
        gb = sb("gamma_beta", [P, 2 * KD])
        warm = sb("warm", [P, S], mybir.dt.bfloat16)
        NS = len(STATS)
        bn = sb("bn", [P, NS * NT, 6])
        mv = sb("mean_var", [P, NS * NT, 2])
        ve = sb("var_eps", [P, NS * NT])
        rstd = sb("rstd", [P, NS * NT])
        both = sb("both_norms", [P, B, 2, NT])
        minus_half = sb("minus_half", [P, NT])
        pos = sb("pos", [P, 6])
        soft = sb("soft_stats", [P, B * NT, 3])

        ring = ctx.enter_context(nc.psum_tensor("ring", [P, 4, 512], F32))
        acc = ctx.enter_context(nc.psum_tensor("acc", [P, 4, 512], F32))

        x_in = [[sem(f"x_in{b}{t}") for t in range(NT)] for b in range(B)]
        w13_in = [sem(f"w13_in{c}") for c in range(NC)]
        w2_in, expand_in, proj_in = sem("w2_in"), sem("expand_in"), sem("proj_in")
        const_in, gb_in, pos_in, out_done = sem("const_in"), sem("gb_in"), sem("pos_in"), sem("out_done")
        ring_full, acc_full = sem("ring_full"), sem("acc_full")
        w13_hi, w13_lo, first_w13_lo = sem("w13_hi"), sem("w13_lo"), sem("first_w13_lo")
        w2_mixed, w2s_hi, w2s_split = sem("w2_mixed"), sem("w2s_hi"), sem("w2s_split")
        w2_hi, w2_lo, had_ready = sem("w2_hi"), sem("w2_lo"), sem("had_ready")
        att_hi, att_split = sem("att_hi"), sem("att_split")
        act_ready, gate_ready, gate_hi, gate_lo = sem("act_ready"), sem("gate_ready"), sem("gate_hi"), sem("gate_lo")
        bn_done, mv_done, var_ready, rstd_ready = sem("bn_done"), sem("mv_done"), sem("var_ready"), sem("rstd_ready")
        outer_ready, outer_added, normed_ready = sem("outer_ready"), sem("outer_added"), sem("normed_ready")
        both_var_ready, both_ready = sem("both_var_ready"), sem("both_ready")
        affine_even, affine_odd = sem("affine_even"), sem("affine_odd")
        xt_hi, xt_lo = sem("xt_hi"), sem("xt_lo")
        x_done = sem("x_done")
        qk_full, qk_hi, qk_rows = sem("qk_full"), sem("qk_hi"), sem("qk_rows_ready")
        qk_copied = [sem("q_copied"), sem("k_copied")]
        logits_ready, exp_ready = sem("logits_ready"), sem("exp_ready")
        recip_ready, probs_ready = sem("recip_ready"), sem("probs_ready")
        pt_hi, pt_lo, av_hi, av_lo = sem("pt_hi"), sem("pt_lo"), sem("av_hi"), sem("av_lo")
        bias_ready, rel_ready, half_ready = sem("bias_ready"), sem("rel_ready"), sem("half_ready")
        warm_ready, table_ready = sem("warm_ready"), sem("table_ready")
        warm_done = sem("warm_done")
        pos_abs, pos_exp, pos_ln, pos_slope = sem("pos_abs"), sem("pos_exp"), sem("pos_ln"), sem("pos_slope")

        def logits(b, i):
            at = P * (b * sum(range(1, NT + 1)) + sum(range(1, i + 1)))
            return raw[:, at:at + (i + 1) * P]

        def w13_split(c):
            return (first_w13_lo, c + 1) if c < POOL_W13_SPLITS else (w13_lo, c - POOL_W13_SPLITS + 1)

        def full_rows(which):
            return normed[:, which * NT // 2:(which + 1) * NT // 2].rearrange("p t d -> p (t d)")

        def ring_bank(s, n=0):
            return ring[:, (RING[s] + n) % 4]

        def acc_bank(s):
            return acc[:, ACC_PLACES[s] % 4]

        def filled(s):
            return (ring_full, ring_end(s)) if s in RING else (acc_full, ACCS[s] + 1)

        def gate_dst(s, part):
            kind, _, b, i = s
            if kind == "up":
                return HID[:, gate_slot(s), part, :]
            if kind == "loc":
                return HID[:, cat_slot(b, i), part, :]
            return V[:, b, i, part, :]

        def gate_width(s):
            return D if s[0] == "val" else S

        def gate_dst_free(eng, s):
            kind, f, b, i = s
            if kind == "up" and b == 1 and i > 0:
                eng.wait_ge(*filled(("down", f, 0, NT - 1)))
            elif kind == "up" and f == 1:
                held = [r for r in range(B) for e in range(EXP // P) if cat_slot(r, e) == gate_slot(s)]
                eng.wait_ge(*filled(("out", 0, held[0] if held else 0, NT - 1)))
            elif kind == "loc":
                eng.wait_ge(*filled(("down", 0, 0 if (b, i) == (0, 0) else 1, NT - 1)))
            elif kind == "val":
                eng.wait_ge(*filled(("had", 0, 0, 3)))

        def xt_free(eng, s):
            _, n, b, _ = s
            if n:
                last = ("up", 0, b, NC - 1) if n == 1 else ("val", 0, b, NT - 1)
                eng.wait_ge(*filled(last))

        def released_by(s):
            kind, f, b, i = s
            if kind in ("up", "loc", "val"):
                return gate_ready, GATES[s] + 1
            if kind == "t":
                return xt_lo, NORMED[s] + 1
            if kind == "qk":
                return qk_full, 2 * (b + 1)
            if kind == "pt":
                return pt_lo, SOFT[s] + 1
            if kind == "av":
                return av_lo, KD * b + i + 1
            if kind == "had":
                return w2_lo, i + 1
            if kind == "score":
                return logits_ready, NT * b + i + 1
            return x_done, SUMS[s] + 1

        block = ctx.enter_context(nc.Block())

        @block.sync
        def _(sp):
            def load_x(b, t):
                sp.dma_start(X[:, b, t], x_d[b, t * P:(t + 1) * P, :]).then_inc(x_in[b][t], 16)

            def load_w13(c):
                if c >= 4:
                    sp.wait_ge(*w13_split(c - 4))
                sp.dma_start(w13_raw[:, c % 4], w13_d[c]).then_inc(w13_in[c], 16)

            for t in (0, 2):
                load_x(0, t)
            load_w13(0)
            load_w13(1)
            sp.dma_start(w2_raw[:, 0], w2_d).then_inc(w2_in, 16)
            load_w13(2)
            load_w13(3)
            for t in range(NT):
                load_x(1, t)
            sp.dma_start(gb[:], gb_d).then_inc(gb_in, 16)
            sp.dma_start(pos[:, 0:1], pos_d.to_broadcast([P, 1])).then_inc(pos_in, 16)
            for c in range(4, NC):
                load_w13(c)
            sp.wait_ge(w2s_split, 4)
            sp.dma_start(att_raw[:, 0:KD * EXPAND_COLS], expand_d).then_inc(expand_in, 16)
            sp.dma_start(att_raw[:, KD * EXPAND_COLS:KD * EXPAND_COLS + EXP // P * D], proj_d).then_inc(proj_in, 16)
            for b in range(B):
                for which in range(2):
                    have, lack = (slice(h * P // 2, (h + 1) * P // 2) for h in (which, 1 - which))
                    sp.wait_ge(qk_full, 2 * b + which + 1)
                    sp.dma_start(full_rows(which)[lack], full_rows(which)[have]).then_inc(qk_copied[which], 16)
            for b in range(B):
                for t in range(NT):
                    sp.wait_ge(x_done, NT * (4 + b) + t + 1)
                    sp.dma_start(out_d[b, t * P:(t + 1) * P, :], X[:, b, t]).then_inc(out_done, 16)
            sp.wait_ge(out_done, 16 * B * NT)

        @block.gpsimd
        def _(pool):
            nc.gpsimd.memset(minus_half[:], -0.5).then_inc(half_ready, 1)
            nc.gpsimd.memset(warm[:], 0.0).then_inc(warm_ready, 1)
            nc.gpsimd.iota(bias[:], pattern=[[-1, S]], base=S - P, channel_multiplier=1,
                           allow_small_or_imprecise_dtypes=True).then_inc(rel_ready, 1)
            pool.wait_ge(half_ready, 1)

            def columns(kind, b):
                return slice(stat(kind, b) * NT, (stat(kind, b) + 1) * NT)

            def reciprocal_roots(kind, b):
                c = columns(kind, b)
                pool.wait_ge(var_ready, roots_made(kind, b))
                nc.gpsimd.tensor_tensor(rstd[:, c], ve[:, c], minus_half[:], ALU.pow).then_inc(rstd_ready, 1)

            def both_norms_scale(b):
                pool.wait_ge(both_var_ready, b + 1)
                nc.gpsimd.tensor_tensor(both[:, b, 1], both[:, b, 0], minus_half[:], ALU.pow).then_inc(both_ready, 1)

            def add_outer(b):
                pool.wait_ge(rstd_ready, roots_made("attention", b))
                for t in range(NT):
                    n, c = NT * b + t, stat("attention", b) * NT + t
                    if n >= 2:
                        pool.wait_ge(outer_added, n - 1)
                    nc.gpsimd.tensor_scalar(outer[:, t % 2], X[:, b, t], mv[:, c, 0:1], rstd[:, c:c + 1],
                                            ALU.subtract, ALU.mult).then_inc(outer_ready, 1)
                    pool.wait_ge(outer_ready, n + 1)
                    pool.wait_ge(normed_ready, NORMED[("t", 1, b, t)] + 1)
                    nc.gpsimd.tensor_tensor(X[:, b, t], X[:, b, t], outer[:, t % 2], ALU.add).then_inc(outer_added, 1)

            for pair in range(NT // 2):
                c = slice(2 * pair, 2 * pair + 2)
                pool.wait_ge(var_ready, pair + 1)
                nc.gpsimd.tensor_tensor(rstd[:, c], ve[:, c], minus_half[:, 0:2], ALU.pow).then_inc(rstd_ready, 1)
            for n in range(POOL_W13_SPLITS):
                pool.wait_ge(w13_hi, n + 1)
                nc.gpsimd.tensor_tensor(W13[:, n, 1], w13_raw[:, n], W13[:, n, 0].bitcast(F32),
                                        ALU.subtract).then_inc(first_w13_lo, 1)
            pool.wait_ge(w2_in, 16)
            for stage in range(3):
                h = 1 << stage
                src = w2_raw[:, stage % 2].rearrange("p (g two r) -> p g two r", two=2, r=h * D)
                dst = w2_raw[:, 1 - stage % 2].rearrange("p (g two r) -> p g two r", two=2, r=h * D)
                if stage:
                    pool.wait_ge(w2_mixed, 2 * stage)
                nc.gpsimd.tensor_tensor(dst[:, :, 0], src[:, :, 0], src[:, :, 1], ALU.add).then_inc(w2_mixed, 1)
                nc.gpsimd.tensor_tensor(dst[:, :, 1], src[:, :, 0], src[:, :, 1], ALU.subtract).then_inc(w2_mixed, 1)
                if stage == 1:
                    reciprocal_roots("ffn0", 1)
            for n in range(NC * D // SPLIT):
                pool.wait_ge(w2s_hi, n + 1)
                r = slice(n * SPLIT, (n + 1) * SPLIT)
                nc.gpsimd.tensor_tensor(w2s[:, 1, r], w2_raw[:, 1, r], w2s[:, 0, r].bitcast(F32),
                                        ALU.subtract).then_inc(w2s_split, 1)
            pool.wait_ge(rel_ready, 1)
            pool.wait_ge(pos_slope, 3)
            nc.gpsimd.tensor_scalar(bias[:], bias[:], pos[:, 5:6], None, ALU.mult).then_inc(rel_ready, 1)
            pool.wait_ge(rel_ready, 2)
            nc.gpsimd.affine_select(out=bias[:], in_=bias[:], compare_op=ALU.is_ge, fill=MASKED,
                                    base=S - P, pattern=[[-1, S]], channel_multiplier=1).then_inc(bias_ready, 1)
            for b in range(B):
                both_norms_scale(b)
                reciprocal_roots("attention", b)
                add_outer(b)
            reciprocal_roots("ffn1", 0)
            reciprocal_roots("ffn1", 1)

        @block.scalar
        def _(act):
            for t in (1, 3):
                act.dma_start(X[:, 0, t], x_d[0, t * P:(t + 1) * P, :]).then_inc(x_in[0][t], 16)
            act.dma_start(const[:], const_d).then_inc(const_in, 16)

            def split_w13(c):
                act.wait_ge(w13_in[c], 16)
                nc.scalar.activation(W13[:, c, 0], w13_raw[:, c % 4], ACT.Copy).then_inc(w13_hi, 1)

            def split_w2s(n):
                if n == 0:
                    act.wait_ge(w2_mixed, 6)
                r = slice(n * SPLIT, (n + 1) * SPLIT)
                nc.scalar.activation(w2s[:, 0, r], w2_raw[:, 1, r], ACT.Copy).then_inc(w2s_hi, 1)

            def split_att(n):
                act.wait_ge(expand_in if n < N_EXPAND_SPLITS else proj_in, 16)
                src = att_raw[:, split_columns(n)]
                if n < N_EXPAND_SPLITS:
                    dst = WE[:, 0, split_columns(n)]
                else:
                    m = n - N_EXPAND_SPLITS
                    dst = WP[:, 2 * m:2 * m + 2, 0, :]
                    src = src.rearrange("p (e d) -> p e d", d=D)
                nc.scalar.activation(dst, src, ACT.Copy).then_inc(att_hi, 1)

            def gate_activation(s):
                n, w = GATES[s], gate_width(s)
                act.wait_ge(ring_full, RING[s] + 1)
                if n >= GATE_BUFS:
                    act.wait_ge(gate_lo, n - GATE_BUFS + 1)
                nc.scalar.activation(gated[:, n % GATE_BUFS, 0:w], ring_bank(s)[:, 0:w],
                                     ACT.Silu if s[0] == "up" else ACT.Gelu).then_inc(act_ready, 1)

            def gate_high(s):
                n = GATES[s]
                act.wait_ge(gate_ready, n + 1)
                gate_dst_free(act, s)
                nc.scalar.activation(gate_dst(s, 0), gated[:, n % GATE_BUFS, 0:gate_width(s)], ACT.Copy)\
                    .then_inc(gate_hi, 1)

            def qk_high(b):
                for which in range(2):
                    act.wait_ge(qk_copied[which], 16 * (b + 1))
                    nc.scalar.activation(QKS[:, which], full_rows(which), ACT.Copy).then_inc(qk_hi, 1)

            def position_slope():
                act.wait_ge(pos_abs, 2)
                nc.scalar.activation(pos[:, 2:3], pos[:, 1:2], ACT.Exp, scale=-1.0).then_inc(pos_exp, 1)
                act.wait_ge(pos_exp, 1)
                nc.scalar.activation(pos[:, 3:4], pos[:, 2:3], ACT.Ln, bias=1.0).then_inc(pos_ln, 1)

            def exponentials(b):
                for i in range(NT):
                    n = NT * b + i
                    act.wait_ge(logits_ready, n + 1)
                    row = logits(b, i)
                    nc.scalar.activation(row, row, ACT.Exp, scale=-1.0, bias=soft[:, n, 0:1],
                                         accum_out=soft[:, n, 1:2]).then_inc(exp_ready, 1)

            def transposed_high(s):
                _, f, b, i = s
                xt_free(act, s)
                if f == 1:
                    a = NT * b + i
                    if a % 2 == 0:
                        act.wait_ge(*filled(s))
                        if a >= 2:
                            act.wait_ge(xt_lo, NORMED[s] - 1)
                        for k in range(KD):
                            c = slice(k * P, (k + 1) * P)
                            nc.scalar.activation(hfull[:, 0, c], acc_bank(s)[:, c], ACT.Identity, scale=gb[:, k:k + 1],
                                                 bias=gb[:, KD + k:KD + k + 1]).then_inc(affine_even, 1)
                        act.wait_ge(affine_even, KD * (a // 2 + 1))
                    else:
                        act.wait_ge(affine_odd, KD * (a // 2 + 1))
                    src = hfull[:, a % 2]
                else:
                    act.wait_ge(*filled(s))
                    src = acc_bank(s)[:, 0:D]
                nc.scalar.activation(XT[:, b, 0, :, i * P:(i + 1) * P], src.rearrange("p (k m) -> p k m", k=KD),
                                     ACT.Copy).then_inc(xt_hi, 1)

            act.wait_ge(half_ready, 1)
            nc.scalar.activation(pos[:, 5:6], minus_half[:, 0:1], ACT.Silu).then_inc(table_ready, 1)
            split_w13(0)
            pending = None
            for s in STEPS:
                kind, f, b, i = s
                if pending and not deferred(s):
                    gate_high(pending)
                    pending = None
                if kind in ("up", "loc", "val"):
                    gate_activation(s)
                if kind == "t":
                    if s == ("t", 1, 0, 0):
                        act.wait_ge(gb_in, 16)
                    transposed_high(s)
                    if s == ("t", 0, 0, NT - 1):
                        split_w13(1)
                        split_w13(2)
                if pending:
                    gate_high(pending)
                pending = s if kind in ("up", "loc", "val") else None
                if (kind, f, b) == ("up", 0, 0) and i + 3 < NC:
                    split_w13(i + 3)
                if s == ("up", 0, 0, 2):
                    nc.scalar.activation(HADR[:], had, ACT.Copy).then_inc(had_ready, 1)
                for n in W2S_SPLITS_AFTER.get(s, ()):
                    split_w2s(n)
                for n in ATT_SPLITS_AFTER.get(s, ()):
                    split_att(n)
                if kind == "had":
                    act.wait_ge(*filled(s))
                    nc.scalar.activation(W2[:, 2 * i:2 * i + 2, 0, :],
                                         acc_bank(s).rearrange("p (c d) -> p c d", d=D), ACT.Copy).then_inc(w2_hi, 1)
                if kind == "qk":
                    act.wait_ge(*filled(s))
                    if b:
                        act.wait_ge(*filled(("score", 0, 0, NT - 1)))
                    nc.scalar.activation(full_rows(0)[0:P // 2], acc_bank(s)[0:P // 2], ACT.Copy, scale=-1.0)\
                        .then_inc(qk_full, 1)
                    nc.scalar.activation(full_rows(1)[P // 2:P], acc_bank(s)[P // 2:P], ACT.Copy).then_inc(qk_full, 1)
                if kind == "pt":
                    act.wait_ge(*filled(s))
                    if b:
                        act.wait_ge(*filled(("av", 0, 0, KD - 1)))
                    nc.scalar.activation(PT[:, 0, 0:i + 1, i * P:(i + 1) * P],
                                         acc_bank(s)[:, 0:(i + 1) * P].rearrange("p (j q) -> p j q", q=P),
                                         ACT.Copy).then_inc(pt_hi, 1)
                if kind == "av":
                    act.wait_ge(*filled(s))
                    nc.scalar.activation(HID[:, cat_slot(b, KD + i), 0, :], ring_bank(s), ACT.Copy).then_inc(av_hi, 1)
                if s in QK_ROWS_AFTER:
                    qk_high(QK_ROWS_AFTER[s])
                if s == ("down", 0, 0, 0):
                    position_slope()
                if s == ("score", 0, 0, NT - 1):
                    exponentials(0)
                if s == ("score", 0, 1, NT - 1):
                    exponentials(1)

        @block.vector
        def _(dve):
            def split_w13(c):
                dve.wait_ge(w13_hi, c + 1)
                nc.vector.tensor_tensor(W13[:, c, 1], w13_raw[:, c % 4], W13[:, c, 0].bitcast(F32),
                                        ALU.subtract).then_inc(w13_lo, 1)

            def split_att(n):
                dve.wait_ge(att_hi, n + 1)
                src = att_raw[:, split_columns(n)]
                if n < N_EXPAND_SPLITS:
                    hi, lo = (WE[:, h, split_columns(n)] for h in range(2))
                else:
                    m = n - N_EXPAND_SPLITS
                    hi, lo = (WP[:, 2 * m:2 * m + 2, h, :] for h in range(2))
                    src = src.rearrange("p (e d) -> p e d", d=D)
                nc.vector.tensor_tensor(lo, src, hi.bitcast(F32), ALU.subtract).then_inc(att_split, 1)

            def statistics(kind, b, pair=None):
                first = stat(kind, b) * NT + (2 * pair if pair else 0)
                tiles_of = range(NT) if pair is None else range(2 * pair, 2 * pair + 2)
                for m, t in enumerate(tiles_of):
                    if kind == "ffn0":
                        dve.wait_ge(x_in[b][t], 16)
                    nc.vector.bn_stats(bn[:, first + m], X[:, b, t]).then_inc(bn_done, 1)
                for m in range(len(tiles_of)):
                    dve.wait_ge(bn_done, first + m + 1)
                    nc.vector.bn_aggr(mv[:, first + m], bn[:, first + m]).then_inc(mv_done, 1)
                end = first + len(tiles_of)
                dve.wait_ge(mv_done, end)
                if kind == "attention":
                    nc.vector.tensor_scalar(both[:, b, 0], mv[:, first:end, 1], 1.0 + EPS, EPS * EPS,
                                            ALU.mult, ALU.add).then_inc(both_var_ready, 1)
                nc.vector.tensor_scalar(ve[:, first:end], mv[:, first:end, 1], EPS, None, ALU.add)\
                    .then_inc(var_ready, 1)

            def normalize(kind, b, s):
                t = s[3]
                n = stat(kind, b) * NT + t
                normed_free(s)
                scale = both[:, b, 1, t:t + 1] if kind == "attention" else rstd[:, n:n + 1]
                nc.vector.tensor_scalar(normed[:, t], X[:, b, t], mv[:, n, 0:1], scale, ALU.subtract, ALU.mult)\
                    .then_inc(normed_ready, 1)

            def normed_free(s):
                n = NORMED[s]
                if n >= NT:
                    before = next(r for r in NORMED if NORMED[r] == n - NT)
                    dve.wait_ge(*filled(before))

            def ffn_statistics(f, b):
                if f:
                    dve.wait_ge(x_done, SUMS[("out", 0, b, NT - 1)] + 1)
                statistics(f"ffn{f}", b)

            def ffn_normalize(f, b):
                dve.wait_ge(rstd_ready, roots_made(f"ffn{f}", b))
                for t in range(NT):
                    normalize(f"ffn{f}", b, ("t", 2 * f, b, t))

            def attention_statistics(b):
                dve.wait_ge(x_done, SUMS[("down", 0, b, NT - 1)] + 1)
                statistics("attention", b)

            def attention_normalize(b):
                dve.wait_ge(both_ready, b + 1)
                for t in range(NT):
                    normalize("attention", b, ("t", 1, b, t))

            def position_magnitude():
                dve.wait_ge(pos_in, 16)
                nc.vector.tensor_scalar(pos[:, 4:5], pos[:, 0:1], -1.0, None, ALU.mult).then_inc(pos_abs, 1)
                dve.wait_ge(pos_abs, 1)
                nc.vector.tensor_tensor(pos[:, 1:2], pos[:, 0:1], pos[:, 4:5], ALU.max).then_inc(pos_abs, 1)

            def position_slope():
                dve.wait_ge(pos_ln, 1)
                nc.vector.tensor_scalar(pos[:, 4:5], pos[:, 0:1], 0.0, None, ALU.max).then_inc(pos_slope, 1)
                dve.wait_ge(pos_slope, 1)
                nc.vector.tensor_tensor(pos[:, 5:6], pos[:, 4:5], pos[:, 3:4], ALU.add).then_inc(pos_slope, 1)
                dve.wait_ge(pos_slope, 2)
                nc.vector.tensor_scalar(pos[:, 5:6], pos[:, 5:6], 1.0 / SCALE, None, ALU.mult).then_inc(pos_slope, 1)

            def gate(s):
                n, w = GATES[s], gate_width(s)
                linear = ring_bank(s)[:, D:2 * D] if s[0] == "val" else ring_bank(s, 1)
                tile = gated[:, n % GATE_BUFS, 0:w]
                dve.wait_ge(act_ready, n + 1)
                dve.wait_ge(*filled(s))
                nc.vector.tensor_tensor(tile, tile, linear, ALU.mult).then_inc(gate_ready, 1)

            def gate_low(s):
                n = GATES[s]
                tile = gated[:, n % GATE_BUFS, 0:gate_width(s)]
                dve.wait_ge(gate_hi, n + 1)
                nc.vector.tensor_tensor(gate_dst(s, 1), tile, gate_dst(s, 0).bitcast(F32), ALU.subtract)\
                    .then_inc(gate_lo, 1)

            def affine(s):
                a = NT * s[2] + s[3]
                dve.wait_ge(*filled(s))
                if a == 1:
                    dve.wait_ge(gb_in, 16)
                else:
                    dve.wait_ge(xt_lo, NORMED[s] - 1)
                for k in range(KD):
                    c = slice(k * P, (k + 1) * P)
                    nc.vector.tensor_scalar(hfull[:, 1, c], acc_bank(s)[:, c], gb[:, k:k + 1],
                                            gb[:, KD + k:KD + k + 1], ALU.mult, ALU.add).then_inc(affine_odd, 1)
                dve.wait_ge(affine_odd, KD * (a // 2 + 1))

            def transposed_low(s):
                _, f, b, i = s
                n = NORMED[s]
                if f == 1:
                    a = NT * b + i
                    source = hfull[:, a % 2]
                else:
                    source = acc_bank(s)[:, 0:D]
                dve.wait_ge(xt_hi, n + 1)
                c = slice(i * P, (i + 1) * P)
                nc.vector.tensor_tensor(XT[:, b, 1, :, c], source.rearrange("p (k m) -> p k m", k=KD),
                                        XT[:, b, 0, :, c].bitcast(F32), ALU.subtract).then_inc(xt_lo, 1)

            def qk_low(b):
                for which, mask in enumerate((qmask, kmask)):
                    part = QKS[:, which]
                    dve.wait_ge(qk_hi, 2 * b + which + 1)
                    nc.vector.scalar_tensor_tensor(part, part.bitcast(F32), mask, full_rows(which), ALU.mult,
                                                   ALU.add).then_inc(qk_rows, 1)

            def negated_logits(s):
                _, _, b, i = s
                w = (i + 1) * P
                dve.wait_ge(*filled(s))
                if b == 0 and i == 0:
                    dve.wait_ge(bias_ready, 1)
                    dve.wait_ge(*w13_split(NC - 1))
                least = soft[:, NT * b + i, 0:1]
                nc.vector.tensor_tensor_reduce(out=logits(b, i), in0=acc_bank(s)[:, 0:w], in1=bias[:, S - w:S],
                                               scale=SCALE, scalar=MASKED, op0=ALU.add, op1=ALU.min,
                                               accum_out=least).then_inc(logits_ready, 1)

            def probabilities(b, i):
                n = NT * b + i
                row = logits(b, i)
                dve.wait_ge(exp_ready, n + 1)
                nc.vector.reciprocal(soft[:, n, 2:3], soft[:, n, 1:2]).then_inc(recip_ready, 1)
                dve.wait_ge(recip_ready, n + 1)
                nc.vector.tensor_scalar(row, row, soft[:, n, 2:3], None, ALU.mult).then_inc(probs_ready, 1)

            def add_product(s):
                kind, _, b, t = s
                dve.wait_ge(*filled(s))
                if kind == "out":
                    dve.wait_ge(outer_added, NT * b + t + 1)
                nc.vector.tensor_tensor(X[:, b, t], X[:, b, t], acc_bank(s)[:, 0:D], ALU.add).then_inc(x_done, 1)

            for pair in range(NT // 2):
                statistics("ffn0", 0, pair)
            for t in range(NT):
                if t % 2 == 0:
                    dve.wait_ge(rstd_ready, t // 2 + 1)
                normalize("ffn0", 0, ("t", 0, 0, t))

            pending = None
            shifted = set()
            for n, s in enumerate(STEPS):
                kind, f, b, i = s
                if pending and not deferred(s):
                    gate_low(pending)
                    pending = None
                if kind in ("up", "loc", "val"):
                    gate(s)
                if kind == "t":
                    odd = ("t", f, b, i | 1)
                    if f == 1 and (i % 2 or STEPS[n + 1] == odd and s != odd) and odd not in shifted:
                        affine(odd)
                        shifted.add(odd)
                    transposed_low(s)
                    if s == ("t", 0, 0, NT - 1):
                        split_w13(2)
                if pending:
                    gate_low(pending)
                pending = s if kind in ("up", "loc", "val") else None
                if (kind, f, b) == ("up", 0, 0) and i + 3 < NC:
                    split_w13(i + 3)
                if s == ("up", 0, 0, 1):
                    ffn_statistics(0, 1)
                if s == ("up", 0, 0, 2):
                    position_magnitude()
                if s == ("up", 0, 0, 3):
                    ffn_normalize(0, 1)
                if kind == "had":
                    dve.wait_ge(w2_hi, i + 1)
                    nc.vector.tensor_tensor(W2[:, 2 * i:2 * i + 2, 1, :],
                                            acc_bank(s).rearrange("p (c d) -> p c d", d=D),
                                            W2[:, 2 * i:2 * i + 2, 0, :].bitcast(F32), ALU.subtract).then_inc(w2_lo, 1)
                for m in ATT_SPLITS_AFTER.get(s, ()):
                    split_att(m)
                if kind in ("down", "out"):
                    add_product(s)
                if kind == "score":
                    negated_logits(s)
                if kind == "pt":
                    dve.wait_ge(pt_hi, SOFT[s] + 1)
                    high, low = (PT[:, h, 0:i + 1, i * P:(i + 1) * P] for h in range(2))
                    nc.vector.tensor_tensor(low, acc_bank(s)[:, 0:(i + 1) * P].rearrange("p (j q) -> p j q", q=P),
                                            high.bitcast(F32), ALU.subtract).then_inc(pt_lo, 1)
                if kind == "av":
                    dve.wait_ge(av_hi, KD * b + i + 1)
                    high, low = (HID[:, cat_slot(b, KD + i), h, :] for h in range(2))
                    nc.vector.tensor_tensor(low, ring_bank(s), high.bitcast(F32), ALU.subtract).then_inc(av_lo, 1)
                if s in QK_ROWS_AFTER:
                    qk_low(QK_ROWS_AFTER[s])
                if s == ("down", 0, 0, NT - 1):
                    attention_statistics(0)
                if s == ("up", 0, 1, 2):
                    attention_normalize(0)
                if s == ("down", 0, 0, 1):
                    position_slope()
                if s == ("down", 0, 1, NT - 1):
                    attention_statistics(1)
                if s == ("loc", 0, 0, 0):
                    attention_normalize(1)
                if s == ("out", 0, 0, NT - 1):
                    ffn_statistics(1, 0)
                if s == ("av", 0, 1, 0):
                    ffn_normalize(1, 0)
                if s == ("out", 0, 1, NT - 1):
                    ffn_statistics(1, 1)
                if s == ("up", 1, 0, 2):
                    ffn_normalize(1, 1)
                if kind == "score" and i == NT - 1:
                    for t in range(NT):
                        probabilities(b, t)

        @block.tensor
        def _(pe):
            def mm(out, stationary, moving, start, stop):
                return nc.tensor.matmul(out, stationary, moving, start=start, stop=stop)

            def three(out, stationary, moving, start, stop):
                mm(out, stationary(0), moving(0), start, False)
                mm(out, stationary(0), moving(1), False, False)
                return mm(out, stationary(1), moving(0), False, stop)

            def bank_free(s):
                for r in occupants(s):
                    pe.wait_ge(*released_by(r))

            def warm_up(count):
                for _ in range(count):
                    ins = mm(ring[:, 3], warm[:, 0:P], warm[:], True, True)
                ins.then_inc(warm_done, 1)

            pe.wait_ge(warm_ready, 1)
            warm_up(WARM_UP)
            for s in STEPS:
                kind, f, b, i = s
                if kind != "out":
                    bank_free(("out", f, b, i) if kind == "open" else s)
                if kind == "t":
                    if s == ("t", 0, 0, 0):
                        pe.wait_ge(const_in, 16)
                    pe.wait_ge(normed_ready, NORMED[s] + 1)
                    for k in range(KD):
                        c = slice(k * P, (k + 1) * P)
                        ins = nc.tensor.transpose(acc_bank(s)[:, c], normed[:, i, c], ident)
                    ins.then_inc(acc_full, 1)
                    if s == ("t", 0, 0, NT - 1):
                        warm_up(WARM_UP_AFTER_T)
                        pe.wait_ge(warm_done, 2)
                if kind == "up":
                    pe.wait_ge(*w13_split(i))
                    parts = 2 if s == ("up", 0, 0, 0) else 1
                    for part in range(parts):
                        q = slice(part * S // parts, (part + 1) * S // parts)
                        pe.wait_ge(xt_lo, NORMED[("t", 2 * f, b, (part + 1) * NT // parts - 1)] + 1)
                        for w in range(2):
                            for k in range(KD):
                                c = slice((w * KD + k) * P, (w * KD + k + 1) * P)
                                ins = three(ring_bank(s, w)[:, q], lambda h: W13[:, i, h, c],
                                            lambda h: XT[:, b, h, k, q], k == 0, k == KD - 1)
                            if part == parts - 1:
                                ins.then_inc(ring_full, 1)
                if kind == "had":
                    pe.wait_ge(had_ready, 1)
                    pe.wait_ge(w2s_split, i + 1)
                    r = slice(i * SPLIT, (i + 1) * SPLIT)
                    mm(acc_bank(s), HADR[:], w2s[:, 0, r], True, False)
                    mm(acc_bank(s), HADR[:], w2s[:, 1, r], False, True).then_inc(acc_full, 1)
                if kind == "down":
                    t = slice(i * P, (i + 1) * P)
                    for c in range(NC):
                        if (f, b, i) == (0, 0, 0) and c % 2 == 0:
                            pe.wait_ge(w2_lo, c // 2 + 1)
                        if i == 0:
                            pe.wait_ge(gate_lo, GATES[("up", f, b, c)] + 1)
                        slot = gate_slot(("up", f, b, c))
                        ins = three(acc_bank(s)[:, 0:D], lambda h: HID[:, slot, h, t], lambda h: W2[:, c, h],
                                    c == 0, c == NC - 1)
                    ins.then_inc(acc_full, 1)
                if kind in ("qk", "loc", "val"):
                    pe.wait_ge(xt_lo, NORMED[("t", 1, b, NT - 1)] + 1)
                    pe.wait_ge(att_split, N_EXPAND_SPLITS)
                if kind == "qk":
                    for k in range(KD):
                        c = slice(k * EXPAND_COLS + COL_QK, k * EXPAND_COLS + COL_QK + P)
                        ins = three(acc_bank(s), lambda h: WE[:, h, c], lambda h: XT[:, b, h, k], k == 0, k == KD - 1)
                    ins.then_inc(acc_full, 1)
                if kind == "loc":
                    for w in range(2):
                        for k in range(KD):
                            at = k * EXPAND_COLS + COL_LOC + (2 * i + w) * P
                            c = slice(at, at + P)
                            ins = three(ring_bank(s, w), lambda h: WE[:, h, c], lambda h: XT[:, b, h, k],
                                        k == 0, k == KD - 1)
                        ins.then_inc(ring_full, 1)
                if kind == "val":
                    t = slice(i * P, (i + 1) * P)
                    for k in range(KD):
                        c = slice(k * EXPAND_COLS + COL_VAL, k * EXPAND_COLS + COL_VAL + 2 * D)
                        ins = three(ring_bank(s), lambda h: XT[:, b, h, k, t], lambda h: WE[:, h, c],
                                    k == 0, k == KD - 1)
                    ins.then_inc(ring_full, 1)
                if kind == "score":
                    pe.wait_ge(qk_rows, 2 * b + 2)
                    w = (i + 1) * P
                    mm(acc_bank(s)[:, 0:w], QKS[:, 0, i * P:w], QKS[:, 1, 0:w], True, True).then_inc(acc_full, 1)
                if kind == "pt":
                    pe.wait_ge(probs_ready, SOFT[s] + 1)
                    for j in range(i + 1):
                        c = slice(j * P, (j + 1) * P)
                        ins = nc.tensor.transpose(acc_bank(s)[:, c], logits(b, i)[:, c], ident)
                    ins.then_inc(acc_full, 1)
                if kind == "av":
                    pe.wait_ge(pt_lo, NT * (b + 1))
                    pe.wait_ge(gate_lo, GATES[("val", 0, b, NT - 1)] + 1)
                    c = slice(i * P, (i + 1) * P)
                    for j in range(NT):
                        ins = three(ring_bank(s)[:, j * P:S], lambda h: V[:, b, j, h, c],
                                    lambda h: PT[:, h, j, j * P:S], j == 0, j == NT - 1)
                    ins.then_inc(ring_full, 1)
                if kind in ("open", "out"):
                    t = slice(i * P, (i + 1) * P)
                    if kind == "open" and i == 0:
                        pe.wait_ge(gate_lo, GATES[("loc", 0, b, KD - 1)] + 1)
                        pe.wait_ge(att_split, N_EXPAND_SPLITS + N_PROJ_SPLITS)
                    for e in range(KD) if kind == "open" else range(KD, EXP // P):
                        if kind == "out" and i == 0:
                            pe.wait_ge(av_lo, KD * b + e - KD + 1)
                        ins = three(acc_bank(("out", f, b, i))[:, 0:D], lambda h: HID[:, cat_slot(b, e), h, t],
                                    lambda h: WP[:, e, h], e == 0, e == EXP // P - 1)
                    if kind == "out":
                        ins.then_inc(acc_full, 1)


def kernel(L0_attn_x, L0_attn_ln_gamma, L0_attn_ln_beta, L0_attn_expand, L0_attn_project, L0_attn_pos_mult,
           L0_ffn_W1, L0_ffn_W2, L0_ffn_W3):
    import numpy as np
    import concourse.bacc as bacc
    from concourse.bass_utils import run_bass_kernel_spmd

    x = np.ascontiguousarray(L0_attn_x)
    w13 = np.stack([np.asarray(L0_ffn_W1), np.asarray(L0_ffn_W3)]).reshape(2, NC, P, KD, P)
    w13 = np.ascontiguousarray(w13.transpose(1, 4, 0, 3, 2)).reshape(NC, P, 2 * KD * P)
    w2 = np.ascontiguousarray(np.asarray(L0_ffn_W2).reshape(D, NC, P).transpose(2, 1, 0)).reshape(P, NC * D)
    e = np.asarray(L0_attn_expand)
    q, k, lin, pre = e[:QK], e[QK:2 * QK], e[2 * QK:2 * QK + EXP], e[2 * QK + EXP:]
    local = [w[c * P:(c + 1) * P] for c in range(KD) for w in (pre, lin)]
    e = np.concatenate([q] * 2 + [k] * 2 + local + [pre[D:], lin[D:]])
    expand = np.ascontiguousarray(e.reshape(EXPAND_COLS, KD, P).transpose(2, 1, 0)).reshape(P, KD * EXPAND_COLS)
    proj = np.ascontiguousarray(np.asarray(L0_attn_project).reshape(D, EXP // P, P).transpose(2, 1, 0))
    proj = proj.reshape(P, EXP // P * D)
    gb = np.concatenate([np.asarray(L0_attn_ln_gamma).reshape(KD, P), np.asarray(L0_attn_ln_beta).reshape(KD, P)])
    gb = np.ascontiguousarray(gb.T)
    pos = np.asarray(L0_attn_pos_mult).reshape(1, 1)
    hadamard = np.ones((1, 1), np.float32)
    while len(hadamard) < P:
        hadamard = np.block([[hadamard, hadamard], [hadamard, -hadamard]])
    rows = np.arange(P)
    const = np.concatenate([np.eye(P), hadamard * (0.5 * H ** -0.5), -(rows // QK % 2)[:, None],
                            -(rows // (2 * QK))[:, None]], axis=1).astype(np.float32)

    nc = bacc.Bacc("TRN2", target_bir_lowering=False, num_devices=1)
    arrays = {"x": x, "w13": w13, "w2": w2, "expand": expand, "proj": proj, "const": const, "gamma_beta": gb,
              "pos_mult": pos}
    args = [nc.dram_tensor(f"{name}_in", a.shape, mybir.dt.from_np(a.dtype), kind="ExternalInput").ap()
            for name, a in arrays.items()]
    out = nc.dram_tensor("out", x.shape, F32, kind="ExternalOutput").ap()
    build_macaron(nc, *args, out)
    r = run_bass_kernel_spmd(nc, [{f"{name}_in": a for name, a in arrays.items()}], core_ids=[0])
    return r.results[0]["out"]
```
